# Optimizing a Trainium2 kernel written in Bass

```python
import numpy as np
import jax
import jax.numpy as jnp

def _softmax(x, axis=-1):
    return jax.nn.softmax(x, axis=axis)

def _gelu(x):
    return jax.nn.gelu(x, approximate=True)

def _silu(x):
    return jax.nn.silu(x)

def _sigmoid(x):
    return jax.nn.sigmoid(x)

def _layernorm(x, axis=-1, eps=1e-05):
    m = jnp.mean(x, axis=axis, keepdims=True)
    v = jnp.var(x, axis=axis, keepdims=True)
    return (x - m) / jnp.sqrt(v + eps)

def _scatter_add(tgt, idx, src, axis=0):
    return tgt.at[idx].add(src)

def _segment_sum(src, seg, n):
    return jax.ops.segment_sum(src, seg, n)
kernel_name = 'mk_recurrent_d2_jaxref_r8_245671'

def setup_inputs(seed: int=0):
    np.random.seed(seed)
    _w = jnp.asarray

    def _L0_attn_setup():
        import jax, jax.numpy as jnp
        import numpy as np

        def log_g(x):
            return jnp.where(x >= 0, jnp.log(jax.nn.relu(x) + 0.5), -jax.nn.softplus(-x))

        def _reference_tuple_inner(x, W1, b1, W2, b2, init_h):
            B, S, _ = x.shape
            Din = init_h.shape[0]
            proj = x @ W1 + b1
            hidden, forget_gate, input_gate = jnp.split(proj, 3, axis=-1)
            diff = jax.nn.softplus(-forget_gate) - jax.nn.softplus(-input_gate)
            log_coeffs = -jax.nn.softplus(diff)
            log_val_coeffs = -jax.nn.softplus(-diff)
            log_values = log_val_coeffs + log_g(hidden)
            prev_log_hidden = jnp.broadcast_to(log_g(init_h), (B, 1, Din))
            log_values = jnp.concatenate([prev_log_hidden, log_values], axis=1)
            log_coeffs = jnp.pad(log_coeffs, ((0, 0), (1, 0), (0, 0)))
            a_star = jnp.cumsum(log_coeffs, axis=1)
            log_h = a_star + jax.lax.cumlogsumexp(log_values - a_star, axis=1)
            out_h = jnp.exp(log_h[:, -S:])
            next_hidden = out_h[:, -1:]
            next_log_hidden = log_h[:, -1:]
            out = out_h @ W2 + b2
            return (out, next_hidden, next_log_hidden)
        key = jax.random.key(seed)
        ks = jax.random.split(key, 6)
        B, S, D, Din = (4, 512, 128, 256)
        x = jax.random.normal(ks[0], (B, S, D), jnp.float32)
        s1 = 1.0 / np.sqrt(D)
        W1 = jax.random.normal(ks[1], (D, 3 * Din), jnp.float32) * s1
        b1 = jax.random.normal(ks[2], (3 * Din,), jnp.float32) * s1
        b1 = b1.at[Din:2 * Din].add(1.0)
        s2 = 1.0 / np.sqrt(Din)
        W2 = jax.random.normal(ks[3], (Din, D), jnp.float32) * s2
        b2 = jax.random.normal(ks[4], (D,), jnp.float32) * s2
        init_h = jax.random.normal(ks[5], (Din,), jnp.float32)
        return {'x': x, 'W1': W1, 'b1': b1, 'W2': W2, 'b2': b2, 'init_h': init_h}
    _L0_attn_in = _L0_attn_setup()

    def _L0_ffn_setup():
        import jax, jax.numpy as jnp
        import numpy as np
        DIM = 128
        DEPTH = 2
        HEADS = 8
        DIM_HEAD = 64
        WINDOW = 64
        INNER = HEADS * DIM_HEAD
        HID = int(DIM * 4 * 2 / 3)
        B, N = (2, 1024)
        QK_SCALE = 8.0

        def shift_token(t):
            t1, t2 = jnp.split(t, 2, axis=-1)
            t2 = jnp.pad(t2, ((0, 0), (1, 0), (0, 0)))[:, :-1]
            return jnp.concatenate([t1, t2], axis=-1)

        def l2norm(t):
            return t / jnp.clip(jnp.linalg.norm(t, axis=-1, keepdims=True), 1e-12)

        def rotate_half(x):
            x1, x2 = jnp.split(x, 2, axis=-1)
            return jnp.concatenate([-x2, x1], axis=-1)

        def rotary_xpos(q, k):
            n = q.shape[-2]
            half_idx = jnp.arange(0, DIM_HEAD, 2, dtype=jnp.float32)
            inv_freq = 1.0 / 10000.0 ** (half_idx / DIM_HEAD)
            t = jnp.arange(n, dtype=jnp.float32)
            freqs = t[:, None] * inv_freq[None, :]
            freqs = jnp.concatenate([freqs, freqs], axis=-1)
            base = (half_idx + 0.4 * DIM_HEAD) / (1.4 * DIM_HEAD)
            power = (t - n // 2) / float(WINDOW // 2)
            scale = base[None, :] ** power[:, None]
            scale = jnp.concatenate([scale, scale], axis=-1)
            cos, sin = (jnp.cos(freqs), jnp.sin(freqs))
            q = q * cos * scale + rotate_half(q) * sin * scale
            k = k * cos / scale + rotate_half(k) * sin / scale
            return (q, k)

        def local_attention(q, k, v):
            b, h, n, d = q.shape
            w = n // WINDOW
            bq = q.reshape(b, h, w, WINDOW, d) * QK_SCALE
            bk = k.reshape(b, h, w, WINDOW, d)
            bv = v.reshape(b, h, w, WINDOW, d)

            def look_around(t):
                p = jnp.pad(t, ((0, 0), (0, 0), (1, 0), (0, 0), (0, 0)))
                return jnp.concatenate([p[:, :, :w], p[:, :, 1:]], axis=3)
            bk, bv = (look_around(bk), look_around(bv))
            bt = jnp.arange(n).reshape(w, WINDOW)
            btp = jnp.pad(bt, ((1, 0), (0, 0)), constant_values=-1)
            btk = jnp.concatenate([btp[:w], btp[1:]], axis=1)
            sim = jnp.einsum('bhwid,bhwjd->bhwij', bq, bk)
            i = bt[:, :, None]
            j = btk[:, None, :]
            mask = (i < j) | (i > j + WINDOW) | (j == -1)
            sim = jnp.where(mask, -jnp.finfo(sim.dtype).max, sim)
            attn = jax.nn.softmax(sim, axis=-1)
            out = jnp.einsum('bhwij,bhwjd->bhwid', attn, bv)
            return out.reshape(b, h, n, d)

        def _layer(x, wqkv, qs, ksc, wo, lg, lb, w1, b1, w2, b2):
            b, n, _ = x.shape
            h = shift_token(x)
            qkv = h @ wqkv
            q, k, v = jnp.split(qkv, 3, axis=-1)
            to_heads = lambda t: t.reshape(b, n, HEADS, DIM_HEAD).transpose(0, 2, 1, 3)
            q, k, v = (to_heads(q), to_heads(k), to_heads(v))
            q = l2norm(q) * qs
            k = l2norm(k) * ksc
            q, k = rotary_xpos(q, k)
            o = local_attention(q, k, v)
            o = o.transpose(0, 2, 1, 3).reshape(b, n, INNER)
            x = x + o @ wo
            h = shift_token(x)
            mu = h.mean(-1, keepdims=True)
            var = h.var(-1, keepdims=True)
            h = (h - mu) / jnp.sqrt(var + 1e-05) * lg + lb
            h = h @ w1 + b1
            a, g = jnp.split(h, 2, axis=-1)
            h = a * jax.nn.gelu(g, approximate=False)
            x = x + h @ w2 + b2
            return x
        key = jax.random.key(seed)
        ks = jax.random.split(key, 6)
        return {'x': jax.random.normal(ks[0], (B, N, DIM), jnp.float32), 'wqkv': jax.random.normal(ks[1], (DEPTH, DIM, 3 * INNER), jnp.float32) * 0.02, 'q_scale': jnp.ones((DEPTH, DIM_HEAD), jnp.float32), 'k_scale': jnp.ones((DEPTH, DIM_HEAD), jnp.float32), 'wo': jax.random.normal(ks[2], (DEPTH, INNER, DIM), jnp.float32) * 0.02, 'ln_g': jnp.ones((DEPTH, DIM), jnp.float32), 'ln_b': jnp.zeros((DEPTH, DIM), jnp.float32), 'w1': jax.random.normal(ks[3], (DEPTH, DIM, 2 * HID), jnp.float32) * 0.02, 'b1': jnp.zeros((DEPTH, 2 * HID), jnp.float32), 'w2': jax.random.normal(ks[4], (DEPTH, HID, DIM), jnp.float32) * 0.02, 'b2': jnp.zeros((DEPTH, DIM), jnp.float32)}
    _L0_ffn_in = _L0_ffn_setup()

    def _L1_attn_setup():
        import jax, jax.numpy as jnp
        import numpy as np
        KEY_DIM = 16
        key = jax.random.key(seed)
        k1, k2, k3, k4, k5 = jax.random.split(key, 5)
        B, N, D, H, KD, VD = (2, 256, 128, 16, 16, 64)
        return {'x': jax.random.normal(k1, (B, N, D), dtype=jnp.float32), 'query_proj': jax.random.normal(k2, (H, KD, D), dtype=jnp.float32) * 0.02, 'key_proj': jax.random.normal(k3, (H, KD, D), dtype=jnp.float32) * 0.02, 'value_proj': jax.random.normal(k4, (H, VD, D), dtype=jnp.float32) * 0.02, 'output_proj': jax.random.normal(k5, (D, H, VD), dtype=jnp.float32) * 0.02}
    _L1_attn_in = _L1_attn_setup()

    def _L1_ffn_setup():
        import jax, jax.numpy as jnp
        import numpy as np
        SL, BS, HS, FF, E, TOPK = (256, 2, 128, 512, 8, 2)
        key = jax.random.key(seed)
        ks = jax.random.split(key, 6)
        T = SL * BS
        x = jax.random.normal(ks[0], (SL, BS, HS), jnp.float32)
        scores = jax.random.uniform(ks[1], (T, E), jnp.float32)
        expert_weights = jax.random.uniform(ks[2], (T, TOPK), jnp.float32)
        expert_indices = jax.random.randint(ks[3], (T, TOPK), 0, E, jnp.int32)
        w1 = jax.random.normal(ks[4], (E, HS, FF), jnp.float32) * (1.0 / np.sqrt(HS))
        w2 = jax.random.normal(ks[5], (E, FF, HS), jnp.float32) * (1.0 / np.sqrt(FF))
        bias = jnp.zeros((HS,), jnp.float32)
        return dict(x=x, scores=scores, expert_weights=expert_weights, expert_indices=expert_indices, w1=w1, w2=w2, bias=bias)
    _L1_ffn_in = _L1_ffn_setup()
    _d = {'L0_attn_x': _L0_attn_in['x'], 'L0_attn_W1': _L0_attn_in['W1'], 'L0_attn_b1': _L0_attn_in['b1'], 'L0_attn_W2': _L0_attn_in['W2'], 'L0_attn_b2': _L0_attn_in['b2'], 'L0_attn_init_h': _L0_attn_in['init_h'], 'L0_ffn_wqkv': _L0_ffn_in['wqkv'], 'L0_ffn_q_scale': _L0_ffn_in['q_scale'], 'L0_ffn_k_scale': _L0_ffn_in['k_scale'], 'L0_ffn_wo': _L0_ffn_in['wo'], 'L0_ffn_ln_g': _L0_ffn_in['ln_g'], 'L0_ffn_ln_b': _L0_ffn_in['ln_b'], 'L0_ffn_w1': _L0_ffn_in['w1'], 'L0_ffn_b1': _L0_ffn_in['b1'], 'L0_ffn_w2': _L0_ffn_in['w2'], 'L0_ffn_b2': _L0_ffn_in['b2'], 'L1_attn_query_proj': _L1_attn_in['query_proj'], 'L1_attn_key_proj': _L1_attn_in['key_proj'], 'L1_attn_value_proj': _L1_attn_in['value_proj'], 'L1_attn_output_proj': _L1_attn_in['output_proj'], 'L1_ffn_scores': _L1_ffn_in['scores'], 'L1_ffn_expert_weights': _L1_ffn_in['expert_weights'], 'L1_ffn_expert_indices': _L1_ffn_in['expert_indices'], 'L1_ffn_w1': _L1_ffn_in['w1'], 'L1_ffn_w2': _L1_ffn_in['w2'], 'L1_ffn_bias': _L1_ffn_in['bias']}
    _x0 = _d['L0_attn_x']
    _d['L0_attn_x'] = jax.random.normal(jax.random.fold_in(jax.random.key(seed), 1), (16, 512, 128), dtype=_x0.dtype)
    del _x0
    return _d

def reference(L0_attn_x, L0_attn_W1, L0_attn_b1, L0_attn_W2, L0_attn_b2, L0_attn_init_h, L0_ffn_wqkv, L0_ffn_q_scale, L0_ffn_k_scale, L0_ffn_wo, L0_ffn_ln_g, L0_ffn_ln_b, L0_ffn_w1, L0_ffn_b1, L0_ffn_w2, L0_ffn_b2, L1_attn_query_proj, L1_attn_key_proj, L1_attn_value_proj, L1_attn_output_proj, L1_ffn_scores, L1_ffn_expert_weights, L1_ffn_expert_indices, L1_ffn_w1, L1_ffn_w2, L1_ffn_bias):

    def _L0_attn_ref(x, W1, b1, W2, b2, init_h):
        import jax, jax.numpy as jnp
        import numpy as np

        def log_g(x):
            return jnp.where(x >= 0, jnp.log(jax.nn.relu(x) + 0.5), -jax.nn.softplus(-x))

        def _reference_tuple_inner(x, W1, b1, W2, b2, init_h):
            B, S, _ = x.shape
            Din = init_h.shape[0]
            proj = x @ W1 + b1
            hidden, forget_gate, input_gate = jnp.split(proj, 3, axis=-1)
            diff = jax.nn.softplus(-forget_gate) - jax.nn.softplus(-input_gate)
            log_coeffs = -jax.nn.softplus(diff)
            log_val_coeffs = -jax.nn.softplus(-diff)
            log_values = log_val_coeffs + log_g(hidden)
            prev_log_hidden = jnp.broadcast_to(log_g(init_h), (B, 1, Din))
            log_values = jnp.concatenate([prev_log_hidden, log_values], axis=1)
            log_coeffs = jnp.pad(log_coeffs, ((0, 0), (1, 0), (0, 0)))
            a_star = jnp.cumsum(log_coeffs, axis=1)
            log_h = a_star + jax.lax.cumlogsumexp(log_values - a_star, axis=1)
            out_h = jnp.exp(log_h[:, -S:])
            next_hidden = out_h[:, -1:]
            next_log_hidden = log_h[:, -1:]
            out = out_h @ W2 + b2
            return (out, next_hidden, next_log_hidden)
        return _reference_tuple_inner(x, W1, b1, W2, b2, init_h)[0]

    def _L0_ffn_ref(x, wqkv, q_scale, k_scale, wo, ln_g, ln_b, w1, b1, w2, b2):
        import jax, jax.numpy as jnp
        import numpy as np
        DIM = 128
        DEPTH = 2
        HEADS = 8
        DIM_HEAD = 64
        WINDOW = 64
        INNER = HEADS * DIM_HEAD
        HID = int(DIM * 4 * 2 / 3)
        B, N = (2, 1024)
        QK_SCALE = 8.0

        def shift_token(t):
            t1, t2 = jnp.split(t, 2, axis=-1)
            t2 = jnp.pad(t2, ((0, 0), (1, 0), (0, 0)))[:, :-1]
            return jnp.concatenate([t1, t2], axis=-1)

        def l2norm(t):
            return t / jnp.clip(jnp.linalg.norm(t, axis=-1, keepdims=True), 1e-12)

        def rotate_half(x):
            x1, x2 = jnp.split(x, 2, axis=-1)
            return jnp.concatenate([-x2, x1], axis=-1)

        def rotary_xpos(q, k):
            n = q.shape[-2]
            half_idx = jnp.arange(0, DIM_HEAD, 2, dtype=jnp.float32)
            inv_freq = 1.0 / 10000.0 ** (half_idx / DIM_HEAD)
            t = jnp.arange(n, dtype=jnp.float32)
            freqs = t[:, None] * inv_freq[None, :]
            freqs = jnp.concatenate([freqs, freqs], axis=-1)
            base = (half_idx + 0.4 * DIM_HEAD) / (1.4 * DIM_HEAD)
            power = (t - n // 2) / float(WINDOW // 2)
            scale = base[None, :] ** power[:, None]
            scale = jnp.concatenate([scale, scale], axis=-1)
            cos, sin = (jnp.cos(freqs), jnp.sin(freqs))
            q = q * cos * scale + rotate_half(q) * sin * scale
            k = k * cos / scale + rotate_half(k) * sin / scale
            return (q, k)

        def local_attention(q, k, v):
            b, h, n, d = q.shape
            w = n // WINDOW
            bq = q.reshape(b, h, w, WINDOW, d) * QK_SCALE
            bk = k.reshape(b, h, w, WINDOW, d)
            bv = v.reshape(b, h, w, WINDOW, d)

            def look_around(t):
                p = jnp.pad(t, ((0, 0), (0, 0), (1, 0), (0, 0), (0, 0)))
                return jnp.concatenate([p[:, :, :w], p[:, :, 1:]], axis=3)
            bk, bv = (look_around(bk), look_around(bv))
            bt = jnp.arange(n).reshape(w, WINDOW)
            btp = jnp.pad(bt, ((1, 0), (0, 0)), constant_values=-1)
            btk = jnp.concatenate([btp[:w], btp[1:]], axis=1)
            sim = jnp.einsum('bhwid,bhwjd->bhwij', bq, bk)
            i = bt[:, :, None]
            j = btk[:, None, :]
            mask = (i < j) | (i > j + WINDOW) | (j == -1)
            sim = jnp.where(mask, -jnp.finfo(sim.dtype).max, sim)
            attn = jax.nn.softmax(sim, axis=-1)
            out = jnp.einsum('bhwij,bhwjd->bhwid', attn, bv)
            return out.reshape(b, h, n, d)

        def _layer(x, wqkv, qs, ksc, wo, lg, lb, w1, b1, w2, b2):
            b, n, _ = x.shape
            h = shift_token(x)
            qkv = h @ wqkv
            q, k, v = jnp.split(qkv, 3, axis=-1)
            to_heads = lambda t: t.reshape(b, n, HEADS, DIM_HEAD).transpose(0, 2, 1, 3)
            q, k, v = (to_heads(q), to_heads(k), to_heads(v))
            q = l2norm(q) * qs
            k = l2norm(k) * ksc
            q, k = rotary_xpos(q, k)
            o = local_attention(q, k, v)
            o = o.transpose(0, 2, 1, 3).reshape(b, n, INNER)
            x = x + o @ wo
            h = shift_token(x)
            mu = h.mean(-1, keepdims=True)
            var = h.var(-1, keepdims=True)
            h = (h - mu) / jnp.sqrt(var + 1e-05) * lg + lb
            h = h @ w1 + b1
            a, g = jnp.split(h, 2, axis=-1)
            h = a * jax.nn.gelu(g, approximate=False)
            x = x + h @ w2 + b2
            return x
        for l in range(DEPTH):
            x = _layer(x, wqkv[l], q_scale[l], k_scale[l], wo[l], ln_g[l], ln_b[l], w1[l], b1[l], w2[l], b2[l])
        return x

    def _L1_attn_ref(x, query_proj, key_proj, value_proj, output_proj):
        import jax, jax.numpy as jnp
        import numpy as np
        KEY_DIM = 16
        q = jnp.einsum('bnd,hkd->bnhk', x, query_proj)
        k = jnp.einsum('bnd,hkd->bnhk', x, key_proj)
        v = jnp.einsum('bnd,hvd->bnhv', x, value_proj)
        sim = jnp.einsum('bnkh,bmhk->bnhm', q, k)
        scale = jnp.asarray(1.0 / np.sqrt(KEY_DIM), dtype=sim.dtype)
        attn = jax.nn.softmax(sim * scale, axis=1)
        o = jnp.einsum('bnhm,bmhv->bnhv', attn, v)
        return jnp.einsum('bnhv,dhv->bnd', o, output_proj)

    def _L1_ffn_ref(x, scores, expert_weights, expert_indices, w1, w2, bias):
        import jax, jax.numpy as jnp
        import numpy as np
        SL, BS, HS, FF, E, TOPK = (256, 2, 128, 512, 8, 2)
        sl, bs, hs = x.shape
        n_exp = w1.shape[0]
        top_k = expert_indices.shape[-1]
        xf = x.reshape(-1, hs)
        flat_idx = expert_indices.reshape(-1)
        flat_w = expert_weights.reshape(-1)
        order = jnp.argsort(flat_idx)
        tok = order // top_k
        tokens_per_expert = jnp.bincount(flat_idx, length=n_exp).astype(jnp.int32)
        xs = xf[tok]
        h = jax.nn.gelu(jax.lax.ragged_dot(xs, w1, tokens_per_expert), approximate=False)
        ys = jax.lax.ragged_dot(h, w2, tokens_per_expert)
        ys = ys * flat_w[order][:, None]
        out = jnp.zeros_like(xf).at[tok].add(ys)
        return out.reshape(sl, bs, hs) + bias
    x = L0_attn_x
    xn = _layernorm(x, axis=-1)
    s = _L0_attn_ref(xn, L0_attn_W1, L0_attn_b1, L0_attn_W2, L0_attn_b2, L0_attn_init_h)
    g = _silu(_L0_ffn_ref(xn, L0_ffn_wqkv, L0_ffn_q_scale, L0_ffn_k_scale, L0_ffn_wo, L0_ffn_ln_g, L0_ffn_ln_b, L0_ffn_w1, L0_ffn_b1, L0_ffn_w2, L0_ffn_b2))
    x = x + s * g
    xn = _layernorm(x, axis=-1)
    s = _L1_attn_ref(xn, L1_attn_query_proj, L1_attn_key_proj, L1_attn_value_proj, L1_attn_output_proj)
    g = _silu(_L1_ffn_ref(xn, L1_ffn_scores, L1_ffn_expert_weights, L1_ffn_expert_indices, L1_ffn_w1, L1_ffn_w2, L1_ffn_bias))
    x = x + s * g
    return x

_drawn_inputs = setup_inputs


def setup_inputs(seed=0):
    import zlib

    import numpy as np

    out = dict(_drawn_inputs(seed))
    spreads = {'L0_ffn_q_scale': (1.0, 0.6),
     'L0_ffn_k_scale': (1.0, 0.6),
     'L0_ffn_ln_g': (1.0, 0.6),
     'L0_ffn_ln_b': (0.0, 0.8),
     'L0_ffn_b1': (0.0, 0.8),
     'L0_ffn_b2': (0.0, 0.1),
     'L1_ffn_bias': (0.0, 2.0)}
    factors = {'L0_attn_init_h': 4.158,
     'L0_ffn_wqkv': 3.555,
     'L0_ffn_wo': 3.58,
     'L0_ffn_w1': 5.916,
     'L0_ffn_w2': 5.86,
     'L1_attn_query_proj': 8.0,
     'L1_attn_key_proj': 8.0,
     'L1_attn_value_proj': 8.0,
     'L1_attn_output_proj': 8.0,
     'L1_ffn_expert_weights': 8.0,
     'L1_ffn_w1': 8.0,
     'L1_ffn_w2': 8.0}
    for name, (base, spread) in spreads.items():
        noise = np.random.default_rng([zlib.crc32(name.encode()), seed]).standard_normal(out[name].shape)
        drawn = base * np.exp(spread * noise) if base else spread * noise
        out[name] = jnp.asarray(drawn.astype(out[name].dtype))
    for name, factor in factors.items():
        out[name] = (out[name] * factor).astype(out[name].dtype)
    return out
```

```python
from contextlib import ExitStack

import numpy as np

import concourse.bass as bass
from concourse import mybir

F32 = mybir.dt.float32
BF16 = mybir.dt.bfloat16
I32 = mybir.dt.int32
ALU = mybir.AluOpType
ACT = mybir.ActivationFunctionType
X = mybir.AxisListType.X

P = 128
B, N, D = 16, 512, 128
NT = N // P
DIN = 256
JG = DIN // P
DEPTH, HEADS, DH, WIN = 2, 8, 64, 64
PAIRS = HEADS // 2
INNER = HEADS * DH
HID = int(D * 4 * 2 / 3)
JM = 3
ROWS = [P, P, HID - 2 * P]
H1, K1, V1 = 16, 16, 64
G1 = 2
Q_PART = [0, 0, 0, 1, 1, 2]
K_PART = [0, 1, 2, 0, 1, 0]
STACK = len(Q_PART) * K1
GROUPS = H1 // G1
STACK_COUNT = 16 * 2 * len(Q_PART)
E, FF, TOPK = 8, 512, 2
JF = FF // P
EPS = 1e-5
FRESH = 6
EXP_LN = "natural_log_exp_and_others"
MASKED = -1e30
NORM_SHIFT = 16
NORM_LEAST = 1e-24


def constants():
    ident = np.eye(P, dtype=np.float32)
    mean = np.full((P, P), 1.0 / D, np.float32)
    r, s = np.arange(P)[:, None] % WIN, np.arange(P)[None, :]
    band = (s >= r) & (s <= r + WIN)
    masks = [np.where(band & (s >= WIN) if first else band, 0.0, MASKED) for first in (1, 0)]
    masks[0][WIN:] = masks[1][WIN:]
    half = np.arange(0, DH, 2, dtype=np.float32)
    inv = (np.float32(1.0) / np.float32(10000.0) ** (half / np.float32(DH))).astype(np.float32)
    t = np.arange(N, dtype=np.float32)
    freq = np.concatenate([t[:, None] * inv[None, :]] * 2, -1)
    base = (half + np.float32(0.4 * DH)) / np.float32(1.4 * DH)
    scale = base[None, :] ** ((t - N // 2) / np.float32(WIN // 2))[:, None]
    scale = np.concatenate([scale, scale], -1).astype(np.float32)
    sign = np.where(np.arange(DH) < DH // 2, -1.0, 1.0).astype(np.float32)
    cos, sin = np.cos(freq), np.sin(freq) * sign
    tab = np.stack([np.stack([8.0 * cos * scale, cos / scale]), np.stack([8.0 * sin * scale, sin / scale])])
    tab = tab.reshape(2, 2, NT, P, DH).transpose(3, 0, 2, 1, 4).reshape(P, -1)
    return np.ascontiguousarray(np.concatenate([ident, ident - mean, mean, *masks, tab], 1).astype(np.float32))


def norm_steps(k):
    return [("centre", k), ("var", k), ("rstd", k), ("normed", k)]


def attn_steps():
    s = [("shift",)]
    for t in range(NT):
        s += [("q", t), ("k", t), ("v", t), ("w", t)]
        if t:
            s += [("tq", t - 1), ("tk", t - 1)]
        s += [("rot", t)]
    s += [("score", 0), ("tq", NT - 1), ("tk", NT - 1)]
    units = 2 * NT
    for u in range(units + 4):
        if 0 < u < units:
            s += [("score", u)]
        if u < units:
            s += [("prob", u)]
        if 1 <= u <= units:
            s += [("pturn", u - 1)]
        if 2 <= u < units + 2:
            s += [("pv", u - 2)]
        if u >= 4 and u % 2 == 0:
            s += [("oturn", u // 2 - 2), ("wo", u // 2 - 2)]
    return s + [("oturn", NT - 1), ("wo", NT - 1)][0:0]


def post_steps(l):
    s = [("shift",), *norm_steps(l)]
    s += [("g", j) for j in range(JM)] + [("gelu",)] + [("a", j) for j in range(JM)] + [("y",)]
    if l:
        s += [("silu1",), ("silu2",), ("silu3",), *norm_steps("out")] + [("qk", c) for c in range(4)]
    return s


def gru_steps():
    return [(n, j) for j in range(JG) for n in ("in_h", "in_f", "in_i", "g1", "g2", "g3", "g4")] + [("out",)]


def glob_steps():
    s = []
    for h in range(H1 + 1):
        for m in range(4):
            if h < H1:
                s += [("sim", h, m)]
            if h and m == 0:
                s += [("scale_v", h - 1)]
            if h and m == 1:
                s += [("av", h - 1)]
            if h and h % 2 == 0:
                p = h // 2 - 1
                s += {2: [("o", p)], 3: [("oturn", p), ("proj", p)]}.get(m, [])
    half = s.index(("sim", H1 // 2, 0))
    values = [("values", n) for n in range(2 * NT)]
    return values, s[:half], s[half:] + [("gate",), ("store",)]


NORM_MARKS = {
    "centre": {"pe": ["c"], "act": ["sq"], "dve": ["c"]},
    "var": {"pe": ["v"], "act": ["ln"]},
    "rstd": {"act": ["r"], "dve": ["n1", "n2", "n3"]},
    "normed": {"dve": ["r", "n"]},
}
PRE_MARKS = {"x": {"pe": ["x"], "act": ["x"]}, **NORM_MARKS}
GRU_MARKS = {
    "in_h": {"pe": ["p"], "dve": ["m", "r"]},
    "in_f": {"pe": ["p"], "dve": ["f"]},
    "in_i": {"pe": ["p"], "dve": ["i"]},
    "g1": {"dve": ["c"], "pool": ["f", "i"]},
    "g2": {"act": ["m", "e", "lm"], "dve": ["s", "d"]},
    "g3": {"act": ["ld", "rd"], "pool": ["t"]},
    "g4": {"act": ["g"], "dve": ["c", "v", "g", "vg", "h"]},
    "out": {"pe": ["o"], "act": ["o"]},
}
ATTN_MARKS = {
    "shift": {"dve": ["h"]},
    "q": {"pe": ["p"], "act": ["sq", "c"]},
    "k": {"pe": ["p"], "act": ["sq", "c"]},
    "v": {"pe": ["p"], "dve": ["c"]},
    "w": {"pe": ["p"], "act": ["c"]},
    "rot": {"dve": ["ss", "max", "c", "s0", "s1", "n1", "n2", "n3", "inv"], "pool": ["add", "q"], "act": ["ln", "inv"]},
    "tq": {"pe": ["t"], "act": ["t"]},
    "tk": {"pe": ["t"], "act": ["t"]},
    "score": {"pe": ["s"], "dve": ["max", "sub"]},
    "prob": {"act": ["p"]},
    "pturn": {"pe": ["t"], "act": ["t"]},
    "pv": {"pe": ["o"], "dve": ["d", "o"]},
    "oturn": {"pe": ["t"], "act": ["t"]},
    "wo": {"pe": ["y"], "dve": ["x"]},
}
POST_MARKS = {
    "shift": {"dve": ["h"]},
    **NORM_MARKS,
    "g": {"pe": ["p"], "act": ["g"]},
    "gelu": {"act": ["g"]},
    "a": {"pe": ["p"], "dve": ["a"]},
    "y": {"pe": ["y"], "dve": ["x"]},
    "silu1": {"dve": ["a"], "act": ["e", "l"]},
    "silu2": {"dve": ["d"], "act": ["s"]},
    "silu3": {"dve": ["y"], "pool": ["g", "x"]},
    "qk": {"pe": ["p"], "act": ["p0", "p1"], "dve": ["r", "p2"]},
}
GLOB_MARKS = {
    "values": {"pe": ["p"], "act": ["v"]},
    "sim": {"pe": ["s"], "dve": ["max"], "act": ["e"]},
    "scale_v": {"dve": ["r"], "pool": ["v"]},
    "av": {"pe": ["o"]},
    "o": {"dve": ["o"]},
    "oturn": {"pe": ["t"], "act": ["t"]},
    "proj": {"pe": ["y"]},
    "gate": {"dve": ["g"], "pool": ["x", "g"]},
    "store": {"pe": ["t"], "act": ["t"]},
}
KEEP_MARKS = {"x0": {"pool": ["c"]}, "x1": {"pool": ["c"]}}
STEPS = {
    "pre": [("x",), *norm_steps("in")],
    "gru": gru_steps(),
    "attn0": attn_steps(),
    "attn1": attn_steps(),
    "post0": post_steps(0),
    "post1": post_steps(1),
    "glob": sum(glob_steps(), []),
    "keep0": [("x0",)],
    "keep1": [("x1",)],
}
MARKS = {"pre": PRE_MARKS, "gru": GRU_MARKS, "attn0": ATTN_MARKS, "attn1": ATTN_MARKS, "post0": POST_MARKS,
         "post1": POST_MARKS, "glob": GLOB_MARKS, "keep0": KEEP_MARKS, "keep1": KEEP_MARKS}


def lane(flow, shift, steps):
    return [(flow, shift, s) for s in steps]


def spread(*lanes):
    at = [((i + 0.5) / len(x), n, i) for n, x in enumerate(lanes) for i in range(len(x))]
    return [lanes[n][i] for _, n, i in sorted(at)]


def loop_order():
    values, first, second = glob_steps()
    cut = STEPS["post1"].index(("silu3",)) + 1
    side = lane("post1", -1, STEPS["post1"][:cut]) + lane("keep0", 0, [("x0",)]) + lane("post1", -1, STEPS["post1"][cut:])
    one = spread(lane("attn0", 0, STEPS["attn0"]), side, lane("glob", -2, second))
    one += lane("keep1", -1, [("x1",)]) + lane("glob", -1, values)
    cut = len(first) // 5
    two = spread(lane("post0", 0, STEPS["post0"]), lane("glob", -1, first[:cut]))
    two += spread(lane("attn1", 0, STEPS["attn1"]), lane("gru", 0, STEPS["gru"]) + lane("pre", 1, STEPS["pre"]),
                  lane("glob", -1, first[cut:]))
    return one, two


class Flow:

    def __init__(self, name, sem):
        self.place, self.per, self.sem = {}, {}, {}
        for e in ("pe", "act", "dve", "pool"):
            order = [(s, m) for s in STEPS[name] for m in MARKS[name][s[0]].get(e, [])]
            if order:
                self.place[e] = {k: i + 1 for i, k in enumerate(order)}
                self.per[e] = len(order)
                self.sem[e] = sem(f"{name}_{e}")


def need(eng, flow, producer, b, step, mark):
    if isinstance(b, int) and b < 0:
        return
    eng.wait_ge(flow.sem[producer], (b + 1) * flow.per[producer] + flow.place[producer][step, mark])


def build(nc, a, out):
    ctx = ExitStack()
    with ctx:
        ctx.enter_context(nc.allow_non_contiguous_dma(reason="bias columns, once, a few KB"))

        def sb(name, shape, dt=F32):
            return ctx.enter_context(nc.sbuf_tensor(name, shape, dt))

        def bank(name):
            return ctx.enter_context(nc.psum_tensor(name, [P, 512], F32))

        def sem(name):
            return ctx.enter_context(nc.semaphore(name))

        flows = {name: Flow(name, sem) for name in STEPS}
        pre, gru, glob, keep0, keep1 = (flows[n] for n in ("pre", "gru", "glob", "keep0", "keep1"))
        attn, post = (flows["attn0"], flows["attn1"]), (flows["post0"], flows["post1"])
        loaded, routing_loaded = sem("weights_loaded"), sem("routing_loaded")
        x_loaded, out_stored = sem("x_loaded"), sem("out_stored")
        parts_stored = [sem("parts_even_stored"), sem("parts_odd_stored")]
        stack_loaded = [sem("stack_even_loaded"), sem("stack_odd_loaded")]
        prep_pe, prep_dve, prep_act, prep_pool = (sem(f"prepared_by_{e}") for e in ("pe", "dve", "act", "pool"))
        expert_loaded, expert_pe, expert_act, expert_dve = (
            sem("expert_loaded"), sem("expert_pe"), sem("expert_act"), sem("expert_dve"))

        const = sb("const", [P, 3 * P])
        ident, centre, mean = const[:, 0:P], const[:, P:2 * P], const[:, 2 * P:3 * P]
        identb = sb("identb", [P, P], BF16)
        masks = sb("masks", [P, 2, 4, P], BF16)
        tab = sb("tab", [P, DEPTH, 2, NT, 2, DH])
        gru_w1 = sb("gru_w1", [P, 3 * DIN])
        gru_b1 = sb("gru_b1", [P, 3, JG])
        gru_w2 = sb("gru_w2", [P, JG, D])
        cols = sb("cols", [P, 64])
        gru_b2, init_h, h0 = cols[:, 0:1], cols[:, 1:3], cols[:, 3:5]
        ln_g, ln_b, mlp_b2 = cols[:, 5:7], cols[:, 7:9], cols[:, 9:11]
        bias1, gate1 = cols[:, 11:12], cols[:, 12:13]
        eps, norm_bias, one = cols[:, 13:14], cols[:, 14:15], cols[:, 15:16]
        b1_raw, b1_eff = cols[:, 16:28].rearrange("p (l j) -> p l j", l=2), cols[:, 28:40].rearrange("p (l j) -> p l j", l=2)
        small = cols[:, 40:52]
        wqkv = sb("wqkv", [P, DEPTH, 3 * INNER])
        wo = sb("wo", [P, DEPTH, PAIRS, D])
        w1 = sb("w1", [P, DEPTH, 2 * HID])
        w2 = sb("w2", [P, DEPTH, JM, D])
        wqk1 = sb("wqk1", [P, 2, H1 * K1])
        wv1 = sb("wv1", [P, H1 * V1])
        wo1 = sb("wo1", [P, H1 // 2, D])
        xin = sb("xin", [P, NT, D])
        x_new, x0, xn0, xn1, x2, x3, gru_o = (
            sb(n, [P, N]) for n in ("x_new", "x0", "xn0", "xn1", "x2", "x3", "gru_o"))
        mlp_in, sq, cent, rstd = (sb(n, [P, N]) for n in ("mlp_in", "sq", "cent", "rstd"))
        mlp_h = sb("mlp_h", [P, JM, N])
        hsh = sb("hsh", [P, WIN + N])
        va, vb = sb("va", [P, NT, HEADS, DH + 1]), sb("vb", [P, NT, HEADS, DH + 1])
        qT, kT = sb("qT", [P, PAIRS, N]), sb("kT", [P, PAIRS, WIN + N])
        stat = sb("stat", [P, 112])
        scratch = sb("scratch", [P, 6144])
        sc = lambda at, n: scratch[:, at:at + n]
        l_sq, l_qk = sc(0, 1024), [sc(1024, 1024), sc(2048, 1024)]
        l_c, l_s, l_q = sc(3072, 1024), sc(4096, 1024), sc(5120, 1024)
        prob = [sc(512 * i, 512).rearrange("p (h n) -> p h n", n=P) for i in range(2)]
        probT = [sc(1024 + 512 * i, 512).rearrange("p (h n) -> p h n", n=P) for i in range(2)]
        o_row, oT = sc(2048, INNER), sc(2560, INNER).rearrange("p (r n) -> p r n", r=PAIRS)
        side = sb("side", [P, 7, N])
        g_c, g_f, g_i, g_m, g_r = (side[:, n, :] for n in range(5))
        g_fi, g_cfi = side[:, 1:3, :], side[:, 0:3, :]
        g_h = [side[:, 5 + j, :] for j in range(JG)]
        s_sig, s_g = side[:, 0, :], side[:, 1, :]
        parts = side[:, 0:3, :].rearrange("p a n -> p (a n)").bitcast(BF16).rearrange("p (c i n) -> p c i n", c=2, i=3)
        rest = [side[:, 3 + i, :] for i in range(2)]
        qs, ks = (sb(n, [STACK, 2, G1, N], BF16) for n in ("qs", "ks"))
        vrow = sb("vrow", [P, NT, H1 * V1])
        ex = sb("ex", [P, 2, 4, N])
        nmax, rsum, rinv = sb("nmax", [P, 8]), sb("rsum", [P, 2, 4]), sb("rinv", [P, 2, 4])
        vsc = sb("vsc", [P, 2, 4, V1])
        o1_row, o1T = sb("o1_row", [P, NT, P]), sb("o1T", [P, N])
        yf = o1_row[:].rearrange("p t n -> p (t n)")
        x1, gate, yrow = (sb(n, [P, N]) for n in ("x1", "gate", "yrow"))
        store = nc.dram_tensor("parts_store", [B, 2, 3, H1 * K1, N], BF16, kind="Internal").ap()

        pb = ctx.enter_context(nc.psum_tensor("pb", [P, 4, 512], F32))
        bank_a, bank_b, bank_c, bank_d = (pb[:, i, :] for i in range(4))
        s_bank = [bank("s0"), bank("s1")]
        o_bank, y_bank = bank("o_bank"), bank("y_bank")

        token_rows = a["L0_attn_x"].rearrange("b (t p) d -> b p t d", p=P)
        out_rows = out.rearrange("b (t p) d -> b p t d", p=P)

        raw_masks = sc(0, 2 * P)
        base_tab = sc(2 * P, 2 * NT * 2 * DH).rearrange("p (c t k d) -> p c t k d", c=2, t=NT, k=2)
        raw_q, raw_k = ex[:, 0, 0, 0:256].rearrange("p (r d) -> p r d", r=2), ex[:, 0, 1, 0:256].rearrange("p (r d) -> p r d", r=2)
        raw_v = ex[:, 0, 2:4, :].rearrange("p a (r d) -> p (a r) d", d=D)
        raw_o = ex[:, 1, 0:2, :].rearrange("p a n -> p (a n)")
        qk_scale = ex[:, 1, 2, 0:4 * DH].rearrange("p (l k d) -> p l k d", l=2, k=2)
        ew = [ex[:, i, 0, :] for i in range(2)]
        ew2 = [ex[:, i, 1, :].rearrange("p (j d) -> p j d", j=JF) for i in range(2)]
        eh = sc(0, JF * N).rearrange("p (j n) -> p j n", j=JF)
        eacc = sc(2048, N).rearrange("p (t d) -> p t d", t=NT)
        ewt = sc(2560, E * NT).rearrange("p (e t) -> p e t", e=E)
        etmp = sc(2600, E * NT * TOPK).rearrange("p (e t k) -> p e t k", e=E, k=TOPK)
        ehf = sc(2700, NT * TOPK).rearrange("p (t k) -> p t k", k=TOPK)
        ews = sc(2720, NT * TOPK).rearrange("p (t k) -> p t k", k=TOPK)
        eidx = scratch[:, 2740:2740 + NT * TOPK].bitcast(I32).rearrange("p (t k) -> p t k", k=TOPK)
        es = [sc(3072 + N * i, N) for i in range(4)]
        col = lambda v: v.rearrange("(j p) -> p j", p=P)
        LOADS = [
            (const[:], a["const"][:, 0:3 * P]),
            (sc(0, 2 * P + 2 * NT * 2 * DH), a["const"][:, 3 * P:]),
            (gru_w1[:], a["L0_attn_W1"]),
            (gru_w2[:], a["L0_attn_W2"].rearrange("(j p) d -> p j d", p=P)),
            (wo[:], a["L0_ffn_wo"].rearrange("l (j p) d -> p l j d", p=P)),
            (wqkv[:], a["L0_ffn_wqkv"].rearrange("l p n -> p l n")),
            (w1[:], a["L0_ffn_w1"].rearrange("l p n -> p l n")),
            (raw_q, a["L1_attn_query_proj"].rearrange("h k d -> (h k) d").rearrange("(r p) d -> p r d", p=P)),
            (raw_k, a["L1_attn_key_proj"].rearrange("h k d -> (h k) d").rearrange("(r p) d -> p r d", p=P)),
            (raw_v, a["L1_attn_value_proj"].rearrange("h k d -> (h k) d").rearrange("(r p) d -> p r d", p=P)),
            (raw_o, a["L1_attn_output_proj"].rearrange("d h v -> d (h v)")),
            (gru_b2, col(a["L0_attn_b2"])),
            (init_h, col(a["L0_attn_init_h"])),
            (bias1, col(a["L1_ffn_bias"])),
            (ln_g, a["L0_ffn_ln_g"].rearrange("l p -> p l")),
            (ln_b, a["L0_ffn_ln_b"].rearrange("l p -> p l")),
            (mlp_b2, a["L0_ffn_b2"].rearrange("l p -> p l")),
        ]
        for l in range(DEPTH):
            LOADS += [
                (w2[:, l, 0:2, :], a["L0_ffn_w2"][l, 0:2 * P, :].rearrange("(j p) d -> p j d", p=P)),
                (w2[0:ROWS[2], l, 2, :], a["L0_ffn_w2"][l, 2 * P:HID, :]),
                (qk_scale[:, l, 0, :], a["L0_ffn_q_scale"][l:l + 1, :].to_broadcast([P, DH])),
                (qk_scale[:, l, 1, :], a["L0_ffn_k_scale"][l:l + 1, :].to_broadcast([P, DH])),
            ]
            for g in range(2):
                LOADS += [
                    (b1_raw[:, l, 3 * g:3 * g + 2], col(a["L0_ffn_b1"][l, g * HID:g * HID + 2 * P])),
                    (b1_raw[0:ROWS[2], l, 3 * g + 2:3 * g + 3],
                     a["L0_ffn_b1"][l, g * HID + 2 * P:(g + 1) * HID].rearrange("(p o) -> p o", o=1)),
                ]
        for k in range(3):
            LOADS += [(gru_b1[:, k, :], col(a["L0_attn_b1"][k * DIN:(k + 1) * DIN]))]
        N_LOADS = 16 * len(LOADS)

        block = ctx.enter_context(nc.Block())

        @block.sync
        def _(sp):
            for dst, src in LOADS:
                sp.dma_start(dst, src).then_inc(loaded, 16)

            def load_x(b):
                need(sp, pre, "pe", b - 1, ("x",), "x")
                sp.dma_start(xin[:], token_rows[b]).then_inc(x_loaded, 16)

            def store_parts(b):
                for c in range(4):
                    need(sp, post[1], "dve", b, ("qk", c), "p2")
                    sp.dma_start(store[b, c // 2].rearrange("i (r p) n -> p i r n", p=P)[:, :, c % 2, :],
                                 parts[:, c % 2]).then_inc(parts_stored[c % 2], 16)

            def load_stack(b, g):
                if g < 2:
                    need(sp, glob, "pe", b - 1, ("sim", G1 * (g + GROUPS - 2) + G1 - 1, 3), "s")
                else:
                    need(sp, glob, "pe", b, ("sim", G1 * (g - 2) + G1 - 1, 3), "s")
                if g == 0:
                    for p in parts_stored:
                        sp.wait_ge(p, b * 32 + 32)
                for c in range(len(Q_PART)):
                    for dst, which, part in ((qs, 0, Q_PART[c]), (ks, 1, K_PART[c])):
                        src = store[b, which, part, G1 * K1 * g:G1 * K1 * (g + 1), :].rearrange("(h k) n -> k h n", k=K1)
                        sp.dma_start(dst[K1 * c:K1 * (c + 1), g % 2, :, :], src).then_inc(stack_loaded[g % 2], 16)

            def store_out(b):
                need(sp, glob, "act", b, ("store",), "t")
                sp.dma_start(out_rows[b], yrow[:].rearrange("p (t d) -> p t d", t=NT)).then_inc(out_stored, 16)

            def load_experts():
                for e in range(E):
                    if e >= 2:
                        sp.wait_ge(expert_pe, 8 * (e - 1))
                    else:
                        sp.wait_ge(prep_pe, 1)
                        sp.wait_ge(prep_dve, 1)
                    sp.dma_start(ew[e % 2], a["L1_ffn_w1"][e]).then_inc(expert_loaded, 16)
                    sp.dma_start(ew2[e % 2], a["L1_ffn_w2"][e].rearrange("(j p) d -> p j d", p=P)).then_inc(expert_loaded, 16)
                    sp.wait_ge(expert_loaded, 32 * (e + 1))

            def step(i):
                has = lambda b: not isinstance(i, int) or 0 <= b < B
                if has(i + 1):
                    load_x(i + 1)
                if has(i - 2):
                    load_stack(i - 2, 6)
                    load_stack(i - 2, 7)
                if has(i - 1):
                    store_parts(i - 1)
                    load_stack(i - 1, 0)
                    load_stack(i - 1, 1)
                if has(i - 2):
                    store_out(i - 2)
                if isinstance(i, int) and i == 1:
                    load_experts()
                if has(i - 1):
                    for g in range(2, 6):
                        load_stack(i - 1, g)

            load_x(0)
            step(0)
            step(1)
            with sp.Fori(2, B - 1) as i:
                step(i)
            for i in range(B - 1, B + 2):
                step(i)
            sp.wait_ge(out_stored, 16 * B)
            for p in parts_stored:
                sp.wait_ge(p, 32 * B)

        phase1, phase2 = loop_order()

        def run(eng, name, does, expert):
            for f in flows.values():
                if name in f.sem:
                    eng.sem_inc(f.sem[name], f.per[name])

            def steps(i, order):
                n, loop_i = 0, i
                for flow, shift, s in order:
                    if name not in MARKS[flow][s[0]]:
                        continue
                    if not isinstance(i, int) and n % FRESH == 0:
                        copy = eng.alloc_register(f"step_{n}")
                        eng.reg_mov(copy, loop_i)
                        i = eng.snap(copy, donate=True, min_val=2, max_val=B - 2)
                    n += 1
                    if not isinstance(i, int) or 0 <= i + shift < B:
                        b = i + shift if shift > 0 else i - -shift if shift else i
                        does[flow](b, s)

            steps(-1, phase2)
            steps(0, phase1)
            steps(0, phase2)
            steps(1, phase1)
            expert()
            steps(1, phase2)
            with eng.Fori(2, B - 1) as i:
                if name == "act":
                    eng.preload_act_table_set(EXP_LN)
                steps(i, phase1 + phase2)
            for i in range(B - 1, B + 2):
                steps(i, phase1 + phase2)

        @block.tensor
        def _(pe):
            def mm(o, l, r, start=True, stop=True):
                return pe.matmul(o, l, r, start=start, stop=stop, skip_group_check=True)

            pe.wait_ge(loaded, N_LOADS)
            for r in range(2):
                pe.transpose(pb[:, 0, P * r:P * r + P], raw_q[:, r, :], ident)
                pe.transpose(pb[:, 1, P * r:P * r + P], raw_k[:, r, :], ident)
            for r in range(8):
                pe.transpose(pb[:, 2 + r // 4, P * (r % 4):P * (r % 4) + P], raw_v[:, r, :], ident)
            for r in range(8):
                pe.transpose(s_bank[r // 4][:, P * (r % 4):P * (r % 4) + P], raw_o[:, P * r:P * r + P], ident)
            for l in range(DEPTH):
                for g in range(2):
                    for j in range(JM):
                        i = 6 * l + 3 * g + j
                        last = mm(o_bank[0:ROWS[j], i:i + 1], w1[:, l, g * HID + P * j:g * HID + P * j + ROWS[j]],
                                  ln_b[:, l:l + 1])
            last.then_inc(prep_pe, 1)
            pe.wait_ge(prep_dve, 2)
            pe.wait_ge(prep_act, 1)
            pe.wait_ge(prep_pool, 1)

            def norm(f, b, s, src):
                if s[0] == "centre":
                    mm(bank_d, centre, src).then_inc(f.sem["pe"], 1)
                else:
                    need(pe, f, "act", b, ("centre", s[1]), "sq")
                    mm(bank_d, mean, sq[:]).then_inc(f.sem["pe"], 1)

            def pre_does(b, s):
                if s[0] == "x":
                    pe.wait_ge(x_loaded, b * 16 + 16)
                    need(pe, gru, "act", b - 1, ("out",), "o")
                    for t in range(NT):
                        last = pe.transpose(bank_d[:, P * t:P * t + P], xin[:, t, :], ident)
                    last.then_inc(pre.sem["pe"], 1)
                else:
                    if s[0] == "centre":
                        need(pe, pre, "act", b, ("x",), "x")
                    norm(pre, b, s, x_new[:])

            def gru_does(b, s):
                kind = s[0]
                if kind == "out":
                    need(pe, gru, "dve", b, ("g4", 1), "h")
                    mm(bank_d, gru_w2[:, 0, :], g_h[0], stop=False)
                    mm(bank_d, gru_w2[:, 1, :], g_h[1], start=False).then_inc(gru.sem["pe"], 1)
                    return
                j, k = s[1], ("in_h", "in_f", "in_i").index(kind)
                if k:
                    need(pe, gru, "dve", b, *((("in_h", j), "r") if k == 1 else (("in_f", j), "f")))
                elif j:
                    need(pe, gru, "dve", b, ("in_i", j - 1), "i")
                else:
                    need(pe, post[0], "dve", b, ("y",), "x")
                mm(bank_d, gru_w1[:, k * DIN + P * j:k * DIN + P * j + P], xn0[:]).then_inc(gru.sem["pe"], 1)

            def attn_does(l, b, s):
                f, kind = attn[l], s[0]
                before = (attn[0], b) if l else (attn[1], b - 1)
                if kind in ("q", "k", "v", "w"):
                    t = s[1]
                    if kind == "q":
                        if t:
                            need(pe, f, "act", b, ("w", t - 1), "c")
                        else:
                            need(pe, before[0], "dve", before[1], ("score", 2 * NT - 1), "sub")
                            need(pe, f, "dve", b, ("shift",), "h")
                    elif kind == "k":
                        if t >= 2:
                            need(pe, f, "act", b, ("tq", t - 2), "t")
                        elif t:
                            need(pe, f, "act", b, ("k", 0), "c")
                        else:
                            need(pe, before[0], "act", before[1], ("oturn", NT - 1), "t")
                    elif kind == "v":
                        if t >= 2:
                            need(pe, f, "act", b, ("tk", t - 2), "t")
                        elif t:
                            need(pe, f, "dve", b, ("v", 0), "c")
                        else:
                            need(pe, before[0], "dve", before[1], ("wo", NT - 1), "x")
                    else:
                        need(pe, f, "act", b, ("q", t), "c")
                    n = {"q": 0, "k": 1, "v": 2, "w": 2}[kind]
                    at = P * t + (0 if kind == "w" else WIN)
                    dst = {"q": bank_a, "k": bank_b, "v": bank_c, "w": bank_a}[kind]
                    mm(dst, hsh[:, at:at + P], wqkv[:, l, INNER * n:INNER * (n + 1)]).then_inc(f.sem["pe"], 1)
                elif kind in ("tq", "tk"):
                    t, k = s[1], int(kind == "tk")
                    if t < NT - 1:
                        need(pe, f, *(("dve", b, ("v", t + 1), "c") if k else ("act", b, ("k", t + 1), "c")))
                    else:
                        need(pe, f, "act", b, (kind, t - 1), "t")
                    need(pe, f, "pool", b, ("rot", t), "q")
                    for r in range(PAIRS):
                        last = pe.transpose((bank_c if k else bank_b)[:, P * r:P * r + P],
                                            l_q[:, INNER * k + P * r:INNER * k + P * r + P], ident)
                    last.then_inc(f.sem["pe"], 1)
                elif kind == "score":
                    t, par = s[1] // 2, s[1] % 2
                    if s[1]:
                        need(pe, f, "dve", b, ("score", s[1] - 1), "sub")
                    else:
                        need(pe, f, "act", b, ("w", NT - 1), "c")
                    need(pe, f, "act", b, ("tk", t), "t")
                    mm(bank_a, identb[:], masks[:, 0 if t == 0 else 1, :, :].rearrange("p h n -> p (h n)"), stop=False)
                    for r in range(PAIRS):
                        for w in range(2):
                            at = P * t + WIN * w
                            last = mm(bank_a[WIN * w:WIN * w + WIN, P * r:P * r + P],
                                      qT[DH * par:DH * par + DH, r, at:at + WIN], kT[DH * par:DH * par + DH, r, at:at + P],
                                      start=False)
                    last.then_inc(f.sem["pe"], 1)
                elif kind == "pturn":
                    u = s[1]
                    if u == 0:
                        need(pe, f, "act", b, ("tq", NT - 1), "t")
                    elif u >= 4 and u % 2 == 0:
                        need(pe, f, "act", b, ("oturn", u // 2 - 2), "t")
                    else:
                        need(pe, f, "act", b, ("pturn", u - 1), "t")
                    need(pe, f, "act", b, ("prob", u), "p")
                    for r in range(PAIRS):
                        last = pe.transpose(bank_b[:, P * r:P * r + P], prob[u % 2][:, r, :], ident)
                    last.then_inc(f.sem["pe"], 1)
                elif kind == "pv":
                    u = s[1]
                    t, par = u // 2, u % 2
                    if u == 0:
                        need(pe, f, "act", b, ("tk", NT - 1), "t")
                    elif u >= 3 and u % 2 == 1:
                        need(pe, f, "dve", b, ("wo", (u + 1) // 2 - 2), "x")
                    else:
                        need(pe, f, "dve", b, ("pv", u - 1), "o")
                    need(pe, f, "act", b, ("pturn", u), "t")
                    for r in range(PAIRS):
                        for w, v in ((0, vb), (1, va)):
                            last = mm(bank_c[WIN * w:WIN * w + WIN, (DH + 1) * r:(DH + 1) * (r + 1)],
                                      probT[u % 2][:, r, WIN * w:WIN * w + WIN], v[:, t, 2 * r + par, :])
                    last.then_inc(f.sem["pe"], 1)
                elif kind == "oturn":
                    t = s[1]
                    need(pe, f, "act", b, *((("pturn", 2 * t + 3), "t") if t < NT - 1 else (("oturn", t - 1), "t")))
                    need(pe, f, "dve", b, ("pv", 2 * t + 1), "o")
                    for r in range(PAIRS):
                        last = pe.transpose(bank_b[:, P * r:P * r + P], o_row[:, P * r:P * r + P], ident)
                    last.then_inc(f.sem["pe"], 1)
                elif kind == "wo":
                    t = s[1]
                    need(pe, f, "dve", b, ("pv", min(2 * t + 2, 2 * NT - 1)), "o")
                    need(pe, f, "act", b, ("oturn", t), "t")
                    for r in range(PAIRS):
                        last = mm(bank_c[:, 0:P], wo[:, l, r, :], oT[:, r, :], start=(r == 0), stop=(r == PAIRS - 1))
                    last.then_inc(f.sem["pe"], 1)

            def post_does(l, b, s):
                f, kind = post[l], s[0]
                if kind == "centre":
                    if s[1] == "out":
                        need(pe, f, "pool", b, ("silu3",), "x")
                    else:
                        if l == 0:
                            need(pe, post[1], "dve", b - 1, ("qk", 3), "r")
                        elif isinstance(b, int) and b == B - 1:
                            need(pe, gru, "act", b, ("out",), "o")
                        else:
                            need(pe, pre, "dve", b + 1, ("rstd", "in"), "n2")
                        need(pe, f, "dve", b, ("shift",), "h")
                    norm(f, b, s, x3[:] if s[1] == "out" else mlp_in[:])
                elif kind == "var":
                    norm(f, b, s, None)
                elif kind in ("g", "a"):
                    j = s[1]
                    if kind == "g":
                        need(pe, f, *(("act", b, ("g", j - 1), "g") if j else ("dve", b, ("normed", l), "n")))
                    else:
                        need(pe, f, *(("dve", b, ("a", j - 1), "a") if j else ("act", b, ("g", JM - 1), "g")))
                    at = HID * (kind == "g") + P * j
                    mm(bank_d[0:ROWS[j], :], w1[:, l, at:at + ROWS[j]], cent[:]).then_inc(f.sem["pe"], 1)
                elif kind == "y":
                    need(pe, f, "dve", b, ("a", JM - 1), "a")
                    for j in range(JM):
                        last = mm(bank_d, w2[0:ROWS[j], l, j, :], mlp_h[0:ROWS[j], j, :], start=(j == 0), stop=(j == JM - 1))
                    last.then_inc(f.sem["pe"], 1)
                elif kind == "qk":
                    c = s[1]
                    need(pe, f, *(("dve", b, ("qk", c - 1), "r") if c else ("dve", b, ("normed", "out"), "n")))
                    mm(bank_d, wqk1[:, c // 2, P * (c % 2):P * (c % 2) + P], xn1[:]).then_inc(f.sem["pe"], 1)

            def glob_does(b, s):
                kind, GE = s[0], glob.sem["pe"]
                if kind == "values":
                    n = s[1]
                    if n >= 2:
                        need(pe, glob, "act", b, ("values", n - 2), "v")
                    else:
                        need(pe, glob, "act", b - 1, ("sim", H1 - 1, 2 + n), "e")
                    if n == 0:
                        need(pe, post[1], "dve", b, ("normed", "out"), "n")
                    mm(s_bank[n % 2][:], xn1[:, P * (n // 2):P * (n // 2) + P], wv1[:, 512 * (n % 2):512 * (n % 2) + 512])\
                        .then_inc(GE, 1)
                elif kind == "sim":
                    _, h, m = s
                    c = 4 * h + m
                    g = h // G1
                    if m == 0 and h % G1 == 0:
                        pe.wait_ge(stack_loaded[g % 2], (b * (GROUPS // 2) + g // 2 + 1) * STACK_COUNT)
                    if c >= 2:
                        need(pe, glob, "act", b, ("sim", (c - 2) // 4, (c - 2) % 4), "e")
                    else:
                        need(pe, glob, "act", b, ("values", 2 * NT - 2 + c), "v")
                    mm(s_bank[c % 2][:], ks[:, g % 2, h % G1, P * m:P * m + P], qs[:, g % 2, h % G1, :]).then_inc(GE, 1)
                elif kind == "av":
                    h = s[1]
                    need(pe, glob, "pool", b, ("scale_v", h), "v")
                    if h % 2 == 0:
                        if h:
                            need(pe, glob, "act", b, ("oturn", h // 2 - 1), "t")
                        else:
                            need(pe, glob, "act", b - 1, ("oturn", 7), "t")
                    for m in range(4):
                        for t in range(NT):
                            last = mm(o_bank[:, P * t + V1 * (h % 2):P * t + V1 * (h % 2) + V1],
                                      ex[:, h % 2, m, P * t:P * t + P], vsc[:, h % 2, m, :],
                                      start=(m == 0 and t == 0), stop=(m == 3 and t == NT - 1))
                    last.then_inc(GE, 1)
                elif kind == "oturn":
                    need(pe, glob, "dve", b, ("o", s[1]), "o")
                    for t in range(NT):
                        last = pe.transpose(o_bank[:, P * t:P * t + P], o1_row[:, t, :], ident)
                    last.then_inc(GE, 1)
                elif kind == "proj":
                    p = s[1]
                    need(pe, glob, "act", b, ("oturn", p), "t")
                    if p == 0:
                        need(pe, glob, "act", b - 1, ("store",), "t")
                    mm(y_bank[:], wo1[:, p, :], o1T[:], start=(p == 0), stop=(p == 7)).then_inc(GE, 1)
                elif kind == "store":
                    need(pe, glob, "pool", b, ("gate",), "x")
                    for t in range(NT):
                        last = pe.transpose(y_bank[:, P * t:P * t + P], yf[:, P * t:P * t + P], ident)
                    last.then_inc(GE, 1)

            def expert():
                need(pe, attn[0], "dve", 1, ("wo", NT - 1), "x")
                need(pe, post[1], "dve", 0, ("qk", 3), "r")
                need(pe, glob, "act", 0, ("values", 2 * NT - 1), "v")
                n = 0
                for e in range(E):
                    pe.wait_ge(expert_loaded, 32 * (e + 1))
                    for j in range(JF):
                        if e:
                            pe.wait_ge(expert_act, JF * (e - 1) + j + 1)
                        mm(pb[:, j, :], ew[e % 2][:, P * j:P * j + P], xn1[:]).then_inc(expert_pe, 1)
                    for t in range(NT):
                        if t == 0:
                            pe.wait_ge(expert_act, JF * (e + 1))
                        if n >= 2:
                            pe.wait_ge(expert_dve, n - 1)
                        for j in range(JF):
                            last = mm(s_bank[n % 2][:, 0:P], eh[:, j, P * t:P * t + P], ew2[e % 2][:, j, :],
                                      start=(j == 0), stop=(j == JF - 1))
                        last.then_inc(expert_pe, 1)
                        n += 1
                pe.wait_ge(expert_dve, n)
                for t in range(NT):
                    last = pe.transpose(y_bank[:, P * t:P * t + P], eacc[:, t, :], ident)
                last.then_inc(expert_pe, 1)
                pe.wait_ge(expert_dve, n + 1)

            run(pe, "pe", {
                "pre": pre_does, "gru": gru_does, "glob": glob_does,
                "attn0": lambda b, s: attn_does(0, b, s), "attn1": lambda b, s: attn_does(1, b, s),
                "post0": lambda b, s: post_does(0, b, s), "post1": lambda b, s: post_does(1, b, s)}, expert)

        @block.scalar
        def _(act):
            A = nc.scalar.activation
            act.preload_act_table_set(EXP_LN)
            act.wait_ge(prep_pe, 1)
            nc.scalar.activation(wv1[:].rearrange("p (a n) -> p a n", a=2), pb[:, 2:4, :], ACT.Copy)
            for i in range(2):
                last = nc.scalar.activation(wo1[:, 4 * i:4 * i + 4, :].rearrange("p r d -> p (r d)"), s_bank[i][:], ACT.Copy)
            act.wait_ge(prep_dve, 1)
            A(small[:, 3:6], small[:, 0:3], ACT.Exp).then_inc(prep_act, 1)
            act.wait_ge(prep_act, 1)
            A(small[:, 6:9], small[:, 3:6], ACT.Ln, bias=1.0).then_inc(prep_act, 1)
            act.wait_ge(prep_dve, 3)
            A(small[:, 0:3], small[:, 9:12], ACT.Exp).then_inc(prep_act, 1)

            def norm(f, b, s):
                FA, k = f.sem["act"], s[1]
                if s[0] == "centre":
                    need(act, f, "dve", b, s, "c")
                    A(sq[:], cent[:], ACT.Square).then_inc(FA, 1)
                elif s[0] == "var":
                    need(act, f, "pe", b, s, "v")
                    A(rstd[:], bank_d, ACT.Ln, bias=eps).then_inc(FA, 1)
                else:
                    need(act, f, "act", b, ("var", k), "ln")
                    A(rstd[:], rstd[:], ACT.Exp, scale=-0.5).then_inc(FA, 1)

            def pre_does(b, s):
                if s[0] == "x":
                    need(act, pre, "pe", b, s, "x")
                    need(act, keep0, "pool", b - 1, ("x0",), "c")
                    A(x_new[:], bank_d, ACT.Copy).then_inc(pre.sem["act"], 1)
                else:
                    norm(pre, b, s)

            def gru_does(b, s):
                kind, GA = s[0], gru.sem["act"]
                if kind == "g2":
                    need(act, gru, "dve", b, ("in_h", s[1]), "m")
                    A(sq[:], g_m, ACT.Exp).then_inc(GA, 1)
                    need(act, gru, "pool", b, ("g1", s[1]), "i")
                    A(g_cfi, g_cfi, ACT.Exp).then_inc(GA, 1)
                    need(act, gru, "act", b, s, "m")
                    A(sq[:], sq[:], ACT.Ln, bias=1.0).then_inc(GA, 1)
                elif kind == "g3":
                    need(act, gru, "dve", b, ("g2", s[1]), "d")
                    A(g_c, g_c, ACT.Ln).then_inc(GA, 1)
                    need(act, gru, "act", b, s, "ld")
                    A(g_c, g_c, ACT.Exp, scale=-1.0).then_inc(GA, 1)
                elif kind == "g4":
                    need(act, gru, "pool", b, ("g3", s[1]), "t")
                    A(g_m, g_m, ACT.Exp).then_inc(GA, 1)
                elif kind == "out":
                    need(act, gru, "pe", b, s, "o")
                    need(act, post[1], "pool", b - 1, ("silu3",), "g")
                    A(gru_o[:], bank_d, ACT.Identity, bias=gru_b2).then_inc(GA, 1)

            def attn_does(l, b, s):
                f, kind = attn[l], s[0]
                FA = f.sem["act"]
                if kind in ("q", "k"):
                    t, k = s[1], int(kind == "k")
                    src = bank_b if k else bank_a
                    need(act, f, "pe", b, s, "p")
                    if t:
                        need(act, f, "dve", b, ("rot", t - 1), "ss")
                    A(l_sq[:, INNER * k:INNER * (k + 1)], src, ACT.Square).then_inc(FA, 1)
                    if t >= 2:
                        need(act, f, "dve", b, ("rot", t - 2), "s1")
                    A(l_qk[t % 2][:, INNER * k:INNER * (k + 1)], src, ACT.Copy).then_inc(FA, 1)
                elif kind == "w":
                    need(act, f, "pe", b, s, "p")
                    A(vb[:, s[1], :, 0:DH], bank_a.rearrange("p (h d) -> p h d", h=HEADS), ACT.Copy).then_inc(FA, 1)
                elif kind == "rot":
                    need(act, f, "dve", b, s, "max")
                    A(stat[:, 16:32], stat[:, 0:16], ACT.Ln, scale=2.0 ** NORM_SHIFT).then_inc(FA, 1)
                    need(act, f, "act", b, s, "ln")
                    A(stat[:, 32:48], stat[:, 16:32], ACT.Exp, scale=-0.5, bias=norm_bias).then_inc(FA, 1)
                elif kind in ("tq", "tk"):
                    t = s[1]
                    need(act, f, "pe", b, s, "t")
                    if kind == "tq":
                        dst, src = qT[:, :, P * t:P * t + P], bank_b
                    else:
                        dst, src = kT[:, :, WIN + P * t:WIN + P * t + P], bank_c
                    A(dst, src.rearrange("p (r n) -> p r n", r=PAIRS), ACT.Copy).then_inc(FA, 1)
                elif kind == "prob":
                    need(act, f, "dve", b, ("score", s[1]), "sub")
                    A(prob[s[1] % 2], prob[s[1] % 2], ACT.Exp).then_inc(FA, 1)
                elif kind == "pturn":
                    u = s[1]
                    need(act, f, "pe", b, s, "t")
                    if u >= 2:
                        need(act, f, "pe", b, ("pv", u - 2), "o")
                    A(probT[u % 2], bank_b.rearrange("p (r n) -> p r n", r=PAIRS), ACT.Copy).then_inc(FA, 1)
                elif kind == "oturn":
                    need(act, f, "pe", b, s, "t")
                    A(oT, bank_b.rearrange("p (r n) -> p r n", r=PAIRS), ACT.Copy).then_inc(FA, 1)

            def post_does(l, b, s):
                f, kind = post[l], s[0]
                FA = f.sem["act"]
                if kind in ("centre", "var", "rstd"):
                    norm(f, b, s)
                elif kind == "g":
                    j = s[1]
                    r = ROWS[j]
                    need(act, f, "pe", b, s, "p")
                    A(mlp_h[0:r, j, :], bank_d[0:r, :], ACT.Identity, bias=b1_eff[0:r, l, 3 + j:4 + j]).then_inc(FA, 1)
                elif kind == "gelu":
                    need(act, f, "act", b, ("g", JM - 1), "g")
                    A(mlp_h[:, 0:2, :], mlp_h[:, 0:2, :], ACT.Gelu)
                    A(mlp_h[0:ROWS[2], 2, :], mlp_h[0:ROWS[2], 2, :], ACT.Gelu).then_inc(FA, 1)
                    act.preload_act_table_set(EXP_LN)
                elif kind == "silu1":
                    need(act, f, "dve", b, s, "a")
                    A(s_sig, s_sig, ACT.Exp).then_inc(FA, 1)
                    need(act, f, "act", b, s, "e")
                    A(s_sig, s_sig, ACT.Ln, bias=1.0).then_inc(FA, 1)
                elif kind == "silu2":
                    need(act, f, "dve", b, s, "d")
                    A(s_sig, s_sig, ACT.Exp).then_inc(FA, 1)
                elif kind == "qk":
                    c = s[1]
                    need(act, f, "pe", b, s, "p")
                    if c >= 2:
                        act.wait_ge(parts_stored[c % 2], b * 32 + 16)
                    scale = K1 ** -0.5 if c < 2 else 1.0
                    A(parts[:, c % 2, 0, :], bank_d, ACT.Copy, scale=scale).then_inc(FA, 1)
                    need(act, f, "dve", b, s, "r")
                    A(parts[:, c % 2, 1, :], rest[c % 2], ACT.Copy).then_inc(FA, 1)

            def glob_does(b, s):
                kind, GA = s[0], glob.sem["act"]
                if kind == "values":
                    n = s[1]
                    need(act, glob, "pe", b, s, "p")
                    if n == 0:
                        need(act, glob, "pool", b - 1, ("scale_v", H1 - 1), "v")
                    A(vrow[:, n // 2, 512 * (n % 2):512 * (n % 2) + 512], s_bank[n % 2][:], ACT.Copy).then_inc(GA, 1)
                elif kind == "sim":
                    _, h, m = s
                    c = 4 * h + m
                    need(act, glob, "dve", b, s, "max")
                    if m == 0:
                        if h >= 2:
                            need(act, glob, "pe", b, ("av", h - 2), "o")
                        else:
                            need(act, glob, "pe", b - 1, ("av", H1 - 2 + h), "o")
                    A(ex[:, h % 2, m, :], s_bank[c % 2][:], ACT.Exp, bias=nmax[:, c % 8:c % 8 + 1],
                      accum_out=rsum[:, h % 2, m:m + 1]).then_inc(GA, 1)
                elif kind == "oturn":
                    p = s[1]
                    need(act, glob, "pe", b, s, "t")
                    if p:
                        need(act, glob, "pe", b, ("proj", p - 1), "y")
                    A(o1T[:], o_bank[:], ACT.Copy).then_inc(GA, 1)
                elif kind == "store":
                    need(act, glob, "pe", b, s, "t")
                    if not isinstance(b, int) or b > 0:
                        act.wait_ge(out_stored, b * 16)
                    A(yrow[:], y_bank[:], ACT.Copy).then_inc(GA, 1)

            def expert():
                for e in range(E):
                    for j in range(JF):
                        act.wait_ge(expert_pe, 8 * e + j + 1)
                        if e:
                            act.wait_ge(expert_pe, 8 * e)
                        A(eh[:, j, :], pb[:, j, :], ACT.Gelu).then_inc(expert_act, 1)
                act.preload_act_table_set(EXP_LN)
                act.wait_ge(expert_dve, E * NT + 2)
                A(es[2], es[1], ACT.Exp).then_inc(expert_act, 1)
                act.wait_ge(expert_act, E * JF + 1)
                A(es[2], es[2], ACT.Ln, bias=1.0).then_inc(expert_act, 1)
                act.wait_ge(expert_dve, E * NT + 3)
                A(es[3], es[3], ACT.Exp).then_inc(expert_act, 1)

            run(act, "act", {
                "pre": pre_does, "gru": gru_does, "glob": glob_does,
                "attn0": lambda b, s: attn_does(0, b, s), "attn1": lambda b, s: attn_does(1, b, s),
                "post0": lambda b, s: post_does(0, b, s), "post1": lambda b, s: post_does(1, b, s)}, expert)

        @block.vector
        def _(dve):
            V = nc.vector
            dve.wait_ge(loaded, N_LOADS)
            dve.wait_ge(prep_pool, 1)
            V.tensor_copy(identb[:], ident)
            for i in range(2):
                for h in range(4):
                    V.tensor_copy(masks[:, i, h, :], raw_masks[:, i * P:(i + 1) * P])
            H = DH // 2
            for l in range(DEPTH):
                for k in range(2):
                    scl = qk_scale[:, l, k, :].unsqueeze(1).broadcast_to([P, NT, DH])
                    V.tensor_tensor(tab[:, l, 0, :, k, :], base_tab[:, 0, :, k, :], scl, ALU.mult)
                    V.tensor_tensor(tab[:, l, 1, :, k, 0:H], base_tab[:, 1, :, k, 0:H], scl[:, :, H:], ALU.mult)
                    V.tensor_tensor(tab[:, l, 1, :, k, H:], base_tab[:, 1, :, k, H:], scl[:, :, 0:H], ALU.mult)
            V.tensor_scalar(small[:, 0:2], init_h, 0.0, None, ALU.min)
            V.scalar_tensor_tensor(small[:, 2:3], bias1, -1.0, bias1, ALU.mult, ALU.min)
            V.tensor_scalar(h0, init_h, 0.0, None, ALU.max).then_inc(prep_dve, 1)
            dve.wait_ge(prep_pe, 1)
            for r in range(2):
                V.tensor_copy(wqk1[:, 0, :].rearrange("p (k h) -> p h k", h=H1)[:, 8 * r:8 * r + 8, :],
                              pb[:, 0, P * r:P * r + P].rearrange("p (h k) -> p h k", k=K1))
            V.tensor_copy(wqk1[:, 1, :], pb[:, 1, 0:2 * P])
            for l in range(DEPTH):
                for g in range(2):
                    for j in range(JM):
                        i = 3 * g + j
                        V.tensor_tensor(b1_eff[0:ROWS[j], l, i:i + 1], o_bank[0:ROWS[j], 6 * l + i:6 * l + i + 1],
                                        b1_raw[0:ROWS[j], l, i:i + 1], ALU.add)
                last = V.tensor_scalar(w1[:, l, :], w1[:, l, :], ln_g[:, l:l + 1], None, ALU.mult)
            last.then_inc(prep_dve, 1)
            dve.wait_ge(prep_act, 2)
            dve.wait_ge(prep_dve, 2)
            V.tensor_tensor(small[:, 9:11], small[:, 0:2], small[:, 6:8], ALU.subtract)
            V.scalar_tensor_tensor(small[:, 11:12], bias1, 0.0, small[:, 8:9], ALU.min, ALU.subtract).then_inc(prep_dve, 1)
            dve.wait_ge(prep_act, 3)
            V.tensor_tensor(h0, h0, small[:, 0:2], ALU.add)
            V.tensor_tensor(gate1, bias1, small[:, 2:3], ALU.mult).then_inc(prep_dve, 1)

            def norm(f, b, s, dst):
                FV, k = f.sem["dve"], s[1]
                if s[0] == "centre":
                    need(dve, f, "pe", b, s, "c")
                    V.tensor_copy(cent[:], bank_d).then_inc(FV, 1)
                elif s[0] == "rstd":
                    need(dve, f, "act", b, s, "r")
                    V.tensor_tensor(sq[:], rstd[:], rstd[:], ALU.mult).then_inc(FV, 1)
                    need(dve, f, "dve", b, s, "n1")
                    V.scalar_tensor_tensor(sq[:], bank_d, EPS, sq[:], ALU.add, ALU.mult).then_inc(FV, 1)
                    need(dve, f, "dve", b, s, "n2")
                    V.tensor_scalar(sq[:], sq[:], -0.5, 1.5, ALU.mult, ALU.add).then_inc(FV, 1)
                else:
                    need(dve, f, "dve", b, ("rstd", k), "n3")
                    V.tensor_tensor(rstd[:], rstd[:], sq[:], ALU.mult).then_inc(FV, 1)
                    need(dve, f, "dve", b, s, "r")
                    V.tensor_tensor(dst, cent[:], rstd[:], ALU.mult).then_inc(FV, 1)

            def pre_does(b, s):
                norm(pre, b, s, xn0[:])

            def gru_does(b, s):
                kind, j, GV = s[0], s[1], gru.sem["dve"]
                if kind == "in_h":
                    need(dve, gru, "pe", b, s, "p")
                    bh = gru_b1[:, 0, j:j + 1]
                    if j == 0:
                        need(dve, post[1], "dve", b - 1, ("qk", 3), "p2")
                    else:
                        need(dve, gru, "dve", b, ("g4", j - 1), "h")
                    V.tensor_scalar(g_m, bank_d, bh, 0.0, ALU.add, ALU.min).then_inc(GV, 1)
                    V.tensor_scalar(g_r, bank_d, bh, 0.0, ALU.add, ALU.max).then_inc(GV, 1)
                elif kind == "in_f":
                    need(dve, gru, "pe", b, s, "p")
                    if j == 0 and not (isinstance(b, int) and b == 0):
                        for p in parts_stored:
                            dve.wait_ge(p, b * 32)
                    V.tensor_scalar(g_f, bank_d, gru_b1[:, 1, j:j + 1], None, ALU.add).then_inc(GV, 1)
                elif kind == "in_i":
                    need(dve, gru, "pe", b, s, "p")
                    V.tensor_scalar(g_i, bank_d, gru_b1[:, 2, j:j + 1], None, ALU.add).then_inc(GV, 1)
                elif kind == "g1":
                    need(dve, gru, "dve", b, ("in_i", j), "i")
                    V.scalar_tensor_tensor(g_c, g_f, 0.0, g_i, ALU.min, ALU.min).then_inc(GV, 1)
                elif kind == "g2":
                    need(dve, gru, "act", b, s, "e")
                    V.tensor_tensor(g_fi, g_fi, side[:, 0:1, :].broadcast_to([P, 2, N]), ALU.add).then_inc(GV, 1)
                    need(dve, gru, "dve", b, s, "s")
                    V.tensor_tensor(g_c, g_f, g_i, ALU.add).then_inc(GV, 1)
                elif kind == "g4":
                    need(dve, gru, "act", b, ("g3", j), "rd")
                    V.tensor_tensor(g_i, g_i, g_c, ALU.mult).then_inc(GV, 1)
                    V.tensor_tensor(g_f, g_f, g_c, ALU.mult).then_inc(GV, 1)
                    need(dve, gru, "act", b, s, "g")
                    V.tensor_tensor(g_r, g_r, g_m, ALU.add).then_inc(GV, 1)
                    need(dve, gru, "dve", b, s, "g")
                    V.tensor_tensor(g_f, g_f, g_r, ALU.mult).then_inc(GV, 1)
                    need(dve, gru, "dve", b, s, "vg")
                    V.tensor_tensor_scan(g_h[j], g_i, g_f, h0[:, j:j + 1], ALU.mult, ALU.add).then_inc(GV, 1)

            def attn_does(l, b, s):
                f, kind = attn[l], s[0]
                FV = f.sem["dve"]
                if kind == "shift":
                    if l:
                        need(dve, post[0], "dve", b, ("y",), "x")
                        need(dve, attn[0], "pe", b, ("w", NT - 1), "p")
                    else:
                        need(dve, pre, "dve", b, ("normed", "in"), "n")
                        need(dve, attn[1], "pe", b - 1, ("w", NT - 1), "p")
                    src = x2 if l else xn0
                    V.tensor_copy(hsh[0:64, WIN:], src[0:64, :])
                    V.tensor_copy(hsh[64:P, WIN + 1:], src[64:P, 0:N - 1]).then_inc(FV, 1)
                elif kind == "v":
                    need(dve, f, "pe", b, s, "p")
                    V.tensor_copy(va[:, s[1], :, 0:DH], bank_c.rearrange("p (h d) -> p h d", h=HEADS)).then_inc(FV, 1)
                elif kind == "rot":
                    t = s[1]
                    need(dve, f, "act", b, ("k", t), "sq")
                    V.tensor_reduce(stat[:, 48:64], l_sq.rearrange("p (g d) -> p g d", d=DH), X, ALU.add).then_inc(FV, 1)
                    need(dve, f, "dve", b, s, "ss")
                    if t:
                        need(dve, f, "act", b, ("rot", t - 1), "ln")
                    V.tensor_scalar(stat[:, 0:16], stat[:, 48:64], NORM_LEAST, None, ALU.max).then_inc(FV, 1)
                    need(dve, f, "act", b, ("k", t), "c")
                    if t:
                        need(dve, f, "pool", b, ("rot", t - 1), "add")
                    src = l_qk[t % 2].rearrange("p (k h d) -> p k h d", k=2, d=DH)
                    cos, sin = (tab[:, l, i, t, :, :].unsqueeze(2).broadcast_to([P, 2, HEADS, DH]) for i in range(2))
                    V.tensor_tensor(l_c.rearrange("p (k h d) -> p k h d", k=2, d=DH), src, cos, ALU.mult).then_inc(FV, 1)
                    o = l_s.rearrange("p (k h d) -> p k h d", k=2, d=DH)
                    V.tensor_tensor(o[:, :, :, 0:H], src[:, :, :, H:], sin[:, :, :, 0:H], ALU.mult).then_inc(FV, 1)
                    V.tensor_tensor(o[:, :, :, H:], src[:, :, :, 0:H], sin[:, :, :, H:], ALU.mult).then_inc(FV, 1)
                    need(dve, f, "act", b, s, "inv")
                    if t:
                        need(dve, f, "pool", b, ("rot", t - 1), "q")
                    r, y = stat[:, 32:48], stat[:, 80:96]
                    V.tensor_tensor(y, r, r, ALU.mult).then_inc(FV, 1)
                    need(dve, f, "dve", b, s, "n1")
                    V.tensor_tensor(y, y, stat[:, 0:16], ALU.mult).then_inc(FV, 1)
                    need(dve, f, "dve", b, s, "n2")
                    V.tensor_scalar(y, y, -0.5, 1.5, ALU.mult, ALU.add).then_inc(FV, 1)
                    need(dve, f, "dve", b, s, "n3")
                    V.tensor_tensor(stat[:, 96:112], r, y, ALU.mult).then_inc(FV, 1)
                elif kind == "score":
                    u = s[1]
                    need(dve, f, "pe", b, s, "s")
                    sims, top = bank_a.rearrange("p (h n) -> p h n", n=P), stat[:, 64 + 4 * (u % 2):68 + 4 * (u % 2)]
                    V.tensor_reduce(top, sims, X, ALU.max).then_inc(FV, 1)
                    need(dve, f, "dve", b, s, "max")
                    if u >= 2:
                        need(dve, f, "pe", b, ("pturn", u - 2), "t")
                    V.tensor_tensor(prob[u % 2], sims, top.unsqueeze(2).broadcast_to([P, PAIRS, P]), ALU.subtract).then_inc(FV, 1)
                elif kind == "pv":
                    t, par = s[1] // 2, s[1] % 2
                    need(dve, f, "pe", b, s, "o")
                    o = bank_c[:, 0:PAIRS * (DH + 1)].rearrange("p (h d) -> p h d", d=DH + 1)
                    inv = stat[:, 72:76] if par == 0 else stat[:, 76:80]
                    V.reciprocal(inv, o[:, :, DH]).then_inc(FV, 1)
                    need(dve, f, "dve", b, s, "d")
                    if par == 0 and t:
                        need(dve, f, "pe", b, ("oturn", t - 1), "t")
                    V.tensor_tensor(o_row.rearrange("p (h a d) -> p h a d", a=2, h=PAIRS)[:, :, par, :], o[:, :, 0:DH],
                                    inv.unsqueeze(2).broadcast_to([P, PAIRS, DH]), ALU.mult).then_inc(FV, 1)
                elif kind == "wo":
                    t = s[1]
                    need(dve, f, "pe", b, s, "y")
                    if l and t == 0:
                        need(dve, keep1, "pool", b - 1, ("x1",), "c")
                    dst, src = (x3, x2) if l else (x2, xn0)
                    V.tensor_tensor(dst[:, P * t:P * t + P], bank_c[:, 0:P], src[:, P * t:P * t + P], ALU.add).then_inc(FV, 1)

            def post_does(l, b, s):
                f, kind = post[l], s[0]
                FV, xl = f.sem["dve"], x3 if l else x2
                if kind == "shift":
                    need(dve, attn[l], "dve", b, ("wo", NT - 1), "x")
                    if l:
                        need(dve, post[0], "pe", b, ("centre", 0), "c")
                    else:
                        need(dve, post[1], "pe", b - 1, ("centre", 1), "c")
                    V.tensor_copy(mlp_in[0:64, :], xl[0:64, :])
                    V.tensor_copy(mlp_in[64:P, 1:], xl[64:P, 0:N - 1]).then_inc(FV, 1)
                elif kind in NORM_MARKS:
                    norm(f, b, s, xn1[:] if s[1] == "out" else cent[:])
                elif kind == "a":
                    j = s[1]
                    r = ROWS[j]
                    need(dve, f, "pe", b, s, "p")
                    if j == 0:
                        need(dve, f, "act", b, ("gelu",), "g")
                    V.scalar_tensor_tensor(mlp_h[0:r, j, :], bank_d[0:r, :], b1_eff[0:r, l, j:j + 1],
                                           mlp_h[0:r, j, :], ALU.add, ALU.mult).then_inc(FV, 1)
                elif kind == "y":
                    need(dve, f, "pe", b, s, "y")
                    V.scalar_tensor_tensor(xl[:], bank_d, mlp_b2[:, l:l + 1], xl[:], ALU.add, ALU.add).then_inc(FV, 1)
                elif kind == "silu1":
                    need(dve, f, "dve", b, ("y",), "x")
                    need(dve, gru, "dve", b, ("g4", JG - 1), "h")
                    V.scalar_tensor_tensor(s_sig, x3[:], -1.0, x3[:], ALU.mult, ALU.min).then_inc(FV, 1)
                elif kind == "silu2":
                    need(dve, f, "act", b, ("silu1",), "l")
                    V.scalar_tensor_tensor(s_sig, x3[:], 0.0, s_sig, ALU.min, ALU.subtract).then_inc(FV, 1)
                elif kind == "silu3":
                    need(dve, f, "act", b, ("silu2",), "s")
                    V.tensor_tensor(x3[:], x3[:], s_sig, ALU.mult).then_inc(FV, 1)
                elif kind == "qk":
                    c = s[1]
                    need(dve, f, "act", b, s, "p0")
                    scale = K1 ** -0.5 if c < 2 else 1.0
                    V.scalar_tensor_tensor(rest[c % 2], bank_d, scale, parts[:, c % 2, 0, :], ALU.mult, ALU.subtract).then_inc(FV, 1)
                    need(dve, f, "act", b, s, "p1")
                    V.tensor_tensor(parts[:, c % 2, 2, :], rest[c % 2], parts[:, c % 2, 1, :], ALU.subtract).then_inc(FV, 1)

            def glob_does(b, s):
                kind, GV = s[0], glob.sem["dve"]
                if kind == "sim":
                    _, h, m = s
                    c = 4 * h + m
                    need(dve, glob, "pe", b, s, "s")
                    V.tensor_reduce(nmax[:, c % 8:c % 8 + 1], s_bank[c % 2][:], X, ALU.max, negate=True).then_inc(GV, 1)
                elif kind == "scale_v":
                    h = s[1]
                    need(dve, glob, "act", b, ("sim", h, 3), "e")
                    if h >= 2:
                        need(dve, glob, "pool", b, ("scale_v", h - 2), "v")
                    else:
                        need(dve, glob, "pool", b - 1, ("scale_v", H1 - 2 + h), "v")
                    V.reciprocal(rinv[:, h % 2, :], rsum[:, h % 2, :]).then_inc(GV, 1)
                elif kind == "o":
                    p = s[1]
                    need(dve, glob, "pe", b, ("av", 2 * p + 1), "o")
                    V.tensor_copy(yf, o_bank[:]).then_inc(GV, 1)
                elif kind == "gate":
                    need(dve, glob, "pe", b, ("proj", 7), "y")
                    need(dve, glob, "pool", b - 1, ("gate",), "g")
                    V.tensor_tensor(yf, y_bank[:], gate[:], ALU.mult).then_inc(GV, 1)

            def expert():
                dve.wait_ge(routing_loaded, 32)
                V.tensor_copy(ehf, eidx).then_inc(prep_dve, 1)
                dve.wait_ge(prep_dve, 5)
                for e in range(E):
                    V.scalar_tensor_tensor(etmp[:, e], ehf, float(e), ews, ALU.is_equal, ALU.mult).then_inc(prep_dve, 1)
                dve.wait_ge(prep_dve, 5 + E)
                V.tensor_reduce(ewt, etmp, X, ALU.add).then_inc(prep_dve, 1)
                dve.wait_ge(prep_dve, 6 + E)
                n = 0
                for e in range(E):
                    for t in range(NT):
                        dve.wait_ge(expert_pe, 8 * e + JF + t + 1)
                        src = s_bank[n % 2][:, 0:P]
                        if e == 0:
                            V.tensor_scalar(eacc[:, t, :], src, ewt[:, e, t:t + 1], None, ALU.mult).then_inc(expert_dve, 1)
                        else:
                            dve.wait_ge(expert_dve, n - NT + 1)
                            V.scalar_tensor_tensor(eacc[:, t, :], src, ewt[:, e, t:t + 1], eacc[:, t, :], ALU.mult, ALU.add)\
                                .then_inc(expert_dve, 1)
                        n += 1
                dve.wait_ge(expert_pe, 8 * E + 1)
                V.tensor_scalar(es[0], y_bank[:], bias1, None, ALU.add).then_inc(expert_dve, 1)
                dve.wait_ge(expert_dve, n + 1)
                V.scalar_tensor_tensor(es[1], es[0], -1.0, es[0], ALU.mult, ALU.min).then_inc(expert_dve, 1)
                dve.wait_ge(expert_act, E * JF + 2)
                V.scalar_tensor_tensor(es[3], es[0], 0.0, es[2], ALU.min, ALU.subtract).then_inc(expert_dve, 1)
                dve.wait_ge(expert_act, E * JF + 3)
                V.tensor_tensor(gate[:], es[0], es[3], ALU.mult).then_inc(expert_dve, 1)

            run(dve, "dve", {
                "pre": pre_does, "gru": gru_does, "glob": glob_does,
                "attn0": lambda b, s: attn_does(0, b, s), "attn1": lambda b, s: attn_does(1, b, s),
                "post0": lambda b, s: post_does(0, b, s), "post1": lambda b, s: post_does(1, b, s)}, expert)

        @block.gpsimd
        def _(pool):
            G = nc.gpsimd
            G.memset(eps, EPS)
            G.memset(one, 1.0)
            G.memset(norm_bias, float(0.5 * NORM_SHIFT * np.log(2.0)))
            G.memset(hsh[:, 0:WIN + 1], 0.0)
            G.memset(mlp_in[:, 0:1], 0.0)
            G.memset(kT[:, :, 0:WIN], 0.0)
            G.memset(va[:, :, :, DH:], 1.0)
            G.memset(vb[:, :, :, DH:], 1.0).then_inc(prep_pool, 1)

            def gru_does(b, s):
                j, GP = s[1], gru.sem["pool"]
                if s[0] == "g1":
                    need(pool, gru, "dve", b, s, "c")
                    G.tensor_tensor(g_f, g_c, g_f, ALU.subtract).then_inc(GP, 1)
                    G.tensor_tensor(g_i, g_c, g_i, ALU.subtract).then_inc(GP, 1)
                else:
                    need(pool, gru, "act", b, ("g2", j), "lm")
                    G.tensor_tensor(g_m, g_m, sq[:], ALU.subtract).then_inc(GP, 1)

            def attn_does(l, b, s):
                f, t = attn[l], s[1]
                need(pool, f, "dve", b, s, "s1")
                if t:
                    need(pool, f, "pe", b, ("tk", t - 1), "t")
                G.tensor_tensor(l_q, l_c, l_s, ALU.add).then_inc(f.sem["pool"], 1)
                need(pool, f, "pool", b, s, "add")
                need(pool, f, "dve", b, s, "inv")
                q = l_q.rearrange("p (g d) -> p g d", d=DH)
                G.tensor_tensor(q, q, stat[:, 96:112].unsqueeze(2).broadcast_to([P, 2 * HEADS, DH]), ALU.mult)\
                    .then_inc(f.sem["pool"], 1)

            def post_does(b, s):
                FP = post[1].sem["pool"]
                need(pool, post[1], "dve", b, s, "y")
                need(pool, gru, "act", b, ("out",), "o")
                G.tensor_tensor(s_g, x3[:], gru_o[:], ALU.mult).then_inc(FP, 1)
                need(pool, post[1], "pool", b, s, "g")
                need(pool, keep0, "pool", b, ("x0",), "c")
                G.tensor_tensor(x3[:], s_g, x0[:], ALU.add).then_inc(FP, 1)

            def keep0_does(b, s):
                need(pool, pre, "act", b, ("x",), "x")
                need(pool, post[1], "pool", b - 1, ("silu3",), "x")
                G.tensor_tensor(x0[:], x_new[:], one.to_broadcast([P, N]), ALU.mult).then_inc(keep0.sem["pool"], 1)

            def keep1_does(b, s):
                need(pool, post[1], "pool", b, ("silu3",), "x")
                need(pool, glob, "pool", b - 1, ("gate",), "x")
                G.tensor_tensor(x1[:], x3[:], one.to_broadcast([P, N]), ALU.mult).then_inc(keep1.sem["pool"], 1)

            def glob_does(b, s):
                GP = glob.sem["pool"]
                if s[0] == "scale_v":
                    h = s[1]
                    need(pool, glob, "dve", b, s, "r")
                    if h == 0:
                        need(pool, glob, "act", b, ("values", 2 * NT - 1), "v")
                    if h >= 2:
                        need(pool, glob, "pe", b, ("av", h - 2), "o")
                    else:
                        need(pool, glob, "pe", b - 1, ("av", H1 - 2 + h), "o")
                    G.tensor_tensor(vsc[:, h % 2], vrow[:, :, V1 * h:V1 * h + V1],
                                    rinv[:, h % 2, :].unsqueeze(2).broadcast_to([P, 4, V1]), ALU.mult).then_inc(GP, 1)
                elif s[0] == "gate":
                    need(pool, glob, "dve", b, s, "g")
                    need(pool, keep1, "pool", b, ("x1",), "c")
                    G.tensor_tensor(yf, yf, x1[:], ALU.add).then_inc(GP, 1)
                    G.tensor_copy(gate[:], gate1.to_broadcast([P, N])).then_inc(GP, 1)

            def expert():
                need(pool, attn[0], "dve", 1, ("wo", NT - 1), "x")
                pool.dma_start(eidx, a["L1_ffn_expert_indices"].rearrange("(t p) k -> p t k", p=P)).then_inc(routing_loaded, 16)
                pool.dma_start(ews, a["L1_ffn_expert_weights"].rearrange("(t p) k -> p t k", p=P)).then_inc(routing_loaded, 16)

            run(pool, "pool", {
                "gru": gru_does, "glob": glob_does, "post1": post_does, "keep0": keep0_does, "keep1": keep1_does,
                "attn0": lambda b, s: attn_does(0, b, s), "attn1": lambda b, s: attn_does(1, b, s)}, expert)


_INS = ["L0_attn_x", "L0_attn_W1", "L0_attn_b1", "L0_attn_W2", "L0_attn_b2", "L0_attn_init_h", "L0_ffn_wqkv",
        "L0_ffn_q_scale", "L0_ffn_k_scale", "L0_ffn_wo", "L0_ffn_ln_g", "L0_ffn_ln_b", "L0_ffn_w1", "L0_ffn_b1",
        "L0_ffn_w2", "L0_ffn_b2", "L1_attn_query_proj", "L1_attn_key_proj", "L1_attn_value_proj",
        "L1_attn_output_proj", "L1_ffn_expert_weights", "L1_ffn_expert_indices", "L1_ffn_w1", "L1_ffn_w2",
        "L1_ffn_bias"]


def kernel(**inputs):
    import concourse.bacc as bacc
    from concourse.bass_utils import run_bass_kernel_spmd as launch

    nc = bacc.Bacc("TRN2", target_bir_lowering=False, num_devices=1)
    arrays = {n: np.ascontiguousarray(inputs[n]) for n in _INS}
    arrays["const"] = constants()
    aps = {n: nc.dram_tensor(f"in_{n}", v.shape, mybir.dt.from_np(v.dtype), kind="ExternalInput").ap()
           for n, v in arrays.items()}
    out = nc.dram_tensor("out", (B, N, D), F32, kind="ExternalOutput").ap()
    build(nc, aps, out)
    r = launch(nc, [{f"in_{n}": v for n, v in arrays.items()}], core_ids=[0])
    return r.results[0]["out"]
```

```python
from contextlib import ExitStack

import numpy as np

import concourse.bass as bass
from concourse import mybir

F32 = mybir.dt.float32
BF16 = mybir.dt.bfloat16
I32 = mybir.dt.int32
ALU = mybir.AluOpType
ACT = mybir.ActivationFunctionType
X = mybir.AxisListType.X

P = 128
B, N, D = 16, 512, 128
NT = N // P
DIN = 256
JG = DIN // P
DEPTH, HEADS, DH, WIN = 2, 8, 64, 64
PAIRS = HEADS // 2
INNER = HEADS * DH
HID = int(D * 4 * 2 / 3)
JM = 3
ROWS = [P, P, HID - 2 * P]
H1, K1, V1 = 16, 16, 64
G1 = 2
Q_PART = [0, 0, 0, 1, 1, 2]
K_PART = [0, 1, 2, 0, 1, 0]
STACK = len(Q_PART) * K1
GROUPS = H1 // G1
STACK_COUNT = 16 * 2
Q_STORES = [(0, 0, 1, 3), (3, 1, 1, 2), (5, 2, 1, 1)]
K_STORES = [(0, 0, 3, 1), (3, 0, 2, 1), (5, 0, 1, 1)]
PUT_COUNT = 16 * len(Q_STORES)
E, FF, TOPK = 8, 512, 2
JF = FF // P
EPS = 1e-5
FRESH = 6
EXP_LN = "natural_log_exp_and_others"
MASKED = -1e30
NORM_SHIFT = 16
NORM_LEAST = 1e-24


def constants():
    ident = np.eye(P, dtype=np.float32)
    mean = np.full((P, P), 1.0 / D, np.float32)
    r, s = np.arange(P)[:, None] % WIN, np.arange(P)[None, :]
    band = (s >= r) & (s <= r + WIN)
    masks = [np.where(band & (s >= WIN) if first else band, 0.0, MASKED) for first in (1, 0)]
    masks[0][WIN:] = masks[1][WIN:]
    for m in masks:
        m[:WIN] = np.roll(m[:WIN], WIN, axis=1)
    half = np.arange(0, DH, 2, dtype=np.float32)
    inv = (np.float32(1.0) / np.float32(10000.0) ** (half / np.float32(DH))).astype(np.float32)
    t = np.arange(N, dtype=np.float32)
    freq = np.concatenate([t[:, None] * inv[None, :]] * 2, -1)
    base = (half + np.float32(0.4 * DH)) / np.float32(1.4 * DH)
    scale = base[None, :] ** ((t - N // 2) / np.float32(WIN // 2))[:, None]
    scale = np.concatenate([scale, scale], -1).astype(np.float32)
    sign = np.where(np.arange(DH) < DH // 2, -1.0, 1.0).astype(np.float32)
    cos, sin = np.cos(freq), np.sin(freq) * sign
    tab = np.stack([np.stack([8.0 * cos * scale, cos / scale]), np.stack([8.0 * sin * scale, sin / scale])])
    tab *= -0.5
    tab = tab.reshape(2, 2, NT, P, DH).transpose(3, 0, 2, 1, 4).reshape(P, -1)
    return np.ascontiguousarray(np.concatenate([ident, ident - mean, mean, *masks, tab], 1).astype(np.float32))


def norm_steps(k):
    return [("centre", k), ("var", k), ("rstd", k), ("normed", k)]


def attn_steps():
    s = [("shift",)]
    for t in range(NT):
        s += [("q", t), ("k", t), ("v", t)]
        if t:
            s += [("rot2", t - 1)]
        s += [("vb", t)]
        if t:
            s += [("tq", t - 1), ("tk", t - 1)]
        s += [("rot", t)]
    s += [("score", 0), ("rot2", NT - 1), ("tq", NT - 1), ("tk", NT - 1)]
    units = 2 * NT
    for u in range(units + 4):
        if 0 < u < units:
            s += [("score", u)]
        if u < units:
            s += [("prob", u)]
        if 1 <= u <= units:
            s += [("pturn", u - 1)]
        if 2 <= u < units + 2:
            s += [("pv", u - 2)]
        if u >= 4 and u % 2 == 0:
            s += [("oturn", u // 2 - 2), ("wo", u // 2 - 2)]
    return s


def post_steps(l):
    s = [("shift",), *norm_steps(l)]
    s += [("g", j) for j in range(JM)] + [("gelu",)] + [("a", j) for j in range(JM)] + [("y",)]
    if l:
        s += [("silu1",), ("silu2",), ("silu3",), *norm_steps("out")] + [(n, c) for c in range(4) for n in ("qk", "qk2")]
    return s


def gru_steps():
    return [(n, j) for j in range(JG) for n in ("in_h", "in_f", "in_i", "g1", "g2", "g3", "g4", "g5")] + [("out",)]


def glob_steps():
    s = []
    for h in range(H1 + 1):
        for m in range(4):
            if h < H1:
                s += [("sim", h, m)]
            if h and m == 0:
                s += [("scale_v", h - 1)]
            if h and m == 1:
                s += [("av", h - 1)]
            if h and h % 2 == 0:
                p = h // 2 - 1
                s += {2: [("o", p)], 3: [("proj", p)]}.get(m, [])
    half = s.index(("sim", H1 // 2, 0))
    values = [("values", n) for n in range(2 * NT)]
    return values, s[:half], s[half:] + [("gate",), ("store",)]


NORM_MARKS = {
    "centre": {"pe": ["c"], "act": ["sq"], "dve": ["c"]},
    "var": {"pe": ["v"], "act": ["ln"]},
    "rstd": {"act": ["r"], "dve": ["n1", "n2"]},
    "normed": {"dve": ["r", "n"]},
}
PRE_MARKS = {"x": {"pe": ["x"], "act": ["x"]}, **NORM_MARKS}
GRU_MARKS = {
    "in_h": {"pe": ["p"], "dve": ["m", "r"]},
    "in_f": {"pe": ["p"], "dve": ["f"]},
    "in_i": {"pe": ["p"], "dve": ["i"]},
    "g1": {"dve": ["c"], "pool": ["f", "i"]},
    "g2": {"act": ["e", "m", "lm"], "dve": ["s", "d"]},
    "g3": {"act": ["ld", "rd"], "pool": ["t"]},
    "g4": {"act": ["g"], "dve": ["c", "v"]},
    "g5": {"dve": ["g", "vg", "h"]},
    "out": {"pe": ["o"], "act": ["o"]},
}
ATTN_MARKS = {
    "shift": {"dve": ["h"]},
    "q": {"pe": ["p"], "act": ["sq", "c"]},
    "k": {"pe": ["p"], "act": ["sq", "c"]},
    "v": {"pe": ["p"], "dve": ["c"]},
    "vb": {"act": ["c"]},
    "rot": {"dve": ["ss", "max", "c", "s0", "s1"], "pool": ["add"], "act": ["ln", "inv"]},
    "rot2": {"dve": ["n1", "n2", "inv"], "pool": ["q"]},
    "tq": {"pe": ["t"], "act": ["t"]},
    "tk": {"pe": ["t"], "act": ["t"]},
    "score": {"pe": ["s"], "dve": ["max", "sub"]},
    "prob": {"act": ["p"]},
    "pturn": {"pe": ["t"], "act": ["t"]},
    "pv": {"pe": ["o"], "dve": ["d", "o"]},
    "oturn": {"pe": ["t"], "act": ["t"]},
    "wo": {"pe": ["y"], "dve": ["x"]},
}
POST_MARKS = {
    "shift": {"dve": ["h"]},
    **NORM_MARKS,
    "g": {"pe": ["p"], "act": ["g"]},
    "gelu": {"act": ["g"]},
    "a": {"pe": ["p"], "dve": ["a"]},
    "y": {"pe": ["y"], "dve": ["x"]},
    "silu1": {"dve": ["a"], "act": ["e", "l"]},
    "silu2": {"dve": ["d"], "act": ["s"]},
    "silu3": {"dve": ["y"], "pool": ["g", "x"]},
    "qk": {"pe": ["p"], "act": ["p0"], "dve": ["r"]},
    "qk2": {"act": ["p1"], "dve": ["p2"]},
}
GLOB_MARKS = {
    "values": {"pe": ["p"], "act": ["v"]},
    "sim": {"pe": ["s"], "dve": ["max"], "act": ["e"]},
    "scale_v": {"dve": ["r"], "pool": ["v"]},
    "av": {"pe": ["o"]},
    "o": {"act": ["t"]},
    "proj": {"pe": ["y"]},
    "gate": {"dve": ["g"], "pool": ["x", "g"]},
    "store": {"pe": ["t"], "act": ["t"]},
}
KEEP_MARKS = {"x0": {"pool": ["c"]}, "x1": {"pool": ["c"]}}
STEPS = {
    "pre": [("x",), *norm_steps("in")],
    "gru": gru_steps(),
    "attn0": attn_steps(),
    "attn1": attn_steps(),
    "post0": post_steps(0),
    "post1": post_steps(1),
    "glob": sum(glob_steps(), []),
    "keep0": [("x0",)],
    "keep1": [("x1",)],
}
MARKS = {"pre": PRE_MARKS, "gru": GRU_MARKS, "attn0": ATTN_MARKS, "attn1": ATTN_MARKS, "post0": POST_MARKS,
         "post1": POST_MARKS, "glob": GLOB_MARKS, "keep0": KEEP_MARKS, "keep1": KEEP_MARKS}


def lane(flow, shift, steps):
    return [(flow, shift, s) for s in steps]


def lanes():
    values, first, second = glob_steps()
    return {
        "a": lane("attn0", 0, STEPS["attn0"]) + lane("post0", 0, STEPS["post0"]) + lane("attn1", 0, STEPS["attn1"]),
        "s": lane("post1", -1, STEPS["post1"]) + lane("keep0", 0, [("x0",)]) + lane("gru", 0, STEPS["gru"])
        + lane("pre", 1, STEPS["pre"]),
        "g": lane("glob", -2, second) + lane("keep1", -1, [("x1",)]) + lane("glob", -1, values + first),
    }


ORDER = {
    "pe": ("2g2a3g2a3g2a3gs2gs2a2g3a3g2asas2asgsgs2asa2gsg3a3g3ag2agag2a3gag2a2gs2gaga3gs2agasg2agas3agsag3asaga"
            "gagagaga6g2a2g2ag2a2ga2gs6a2s2g2a2g3a4g8as2g3ags4a2g3a3g3asgag3ag2agag2ag3as2a2g2as2gasga2gsa4ga"),
    "act": ("2ga3ga2g5a2gsg2a2s2a3g2agas3asa2s4a5g5a2gagasgsgag3a3ga4g3sgagas2asa2g2sg2as2a2sgas2ga2g2a6g2agaga2g"
            "6a4g5a2gag7as3a2s2g5a2g2a2g2a2g3agsa2sag2agag2agasgas3gsg2sa4g"),
    "dve": ("a5gas3g3a2gs2ga2g2asgsagag2a2sgs2a3gsga2g2agsa2g2sg2a4ga2gs3g3ag2sagsgasagsasasg2asa2s5a7g5a2gs2as2a"
            "3gags2agsa3g3as2a3sa2g2a3g2asga2sa2g2ags2as2gas2aga3gagasga3g2s2ga"),
    "pool": ("2g2ag3ag3a2gs5gsg2ag2as2ags2agsgs2g"),
}


def merged(engine):
    left = {k: iter([x for x in v if engine in MARKS[x[0]][x[2][0]]]) for k, v in lanes().items()}
    count, steps = "", []
    for c in ORDER[engine]:
        if c.isdigit():
            count += c
        else:
            steps += [next(left[c]) for _ in range(int(count or 1))]
            count = ""
    assert not any(list(x) for x in left.values())
    return steps


class Flow:

    def __init__(self, name, sem):
        self.place, self.per, self.sem = {}, {}, {}
        for e in ("pe", "act", "dve", "pool"):
            order = [(s, m) for s in STEPS[name] for m in MARKS[name][s[0]].get(e, [])]
            if order:
                self.place[e] = {k: i + 1 for i, k in enumerate(order)}
                self.per[e] = len(order)
                self.sem[e] = sem(f"{name}_{e}")


def need(eng, flow, producer, b, step, mark):
    if isinstance(b, int) and b < 0:
        return
    eng.wait_ge(flow.sem[producer], (b + 1) * flow.per[producer] + flow.place[producer][step, mark])


def build(nc, a, out):
    ctx = ExitStack()
    with ctx:
        ctx.enter_context(nc.allow_non_contiguous_dma(reason="bias columns, once, a few KB"))

        def sb(name, shape, dt=F32):
            return ctx.enter_context(nc.sbuf_tensor(name, shape, dt))

        def bank(name):
            return ctx.enter_context(nc.psum_tensor(name, [P, 512], F32))

        def sem(name):
            return ctx.enter_context(nc.semaphore(name))

        flows = {name: Flow(name, sem) for name in STEPS}
        pre, gru, glob, keep0, keep1 = (flows[n] for n in ("pre", "gru", "glob", "keep0", "keep1"))
        attn, post = (flows["attn0"], flows["attn1"]), (flows["post0"], flows["post1"])
        loaded, routing_loaded = sem("weights_loaded"), sem("routing_loaded")
        x_loaded, out_stored = sem("x_loaded"), sem("out_stored")
        parts_stored = [sem("parts_even_stored"), sem("parts_odd_stored")]
        stack_loaded = [sem("stack_even_loaded"), sem("stack_odd_loaded")]
        prep_pe, prep_dve, prep_act, prep_pool = (sem(f"prepared_by_{e}") for e in ("pe", "dve", "act", "pool"))
        expert_loaded, expert_pe, expert_act, expert_dve = (
            sem("expert_loaded"), sem("expert_pe"), sem("expert_act"), sem("expert_dve"))

        const = sb("const", [P, 3 * P])
        ident, centre, mean = const[:, 0:P], const[:, P:2 * P], const[:, 2 * P:3 * P]
        identb = sb("identb", [P, P], BF16)
        masks = sb("masks", [P, 2, 4, P], BF16)
        tab = sb("tab", [P, DEPTH, 2, NT, 2, DH])
        gru_w1 = sb("gru_w1", [P, 3 * DIN])
        gru_b1 = sb("gru_b1", [P, 3, JG])
        gru_w2 = sb("gru_w2", [P, JG, D])
        cols = sb("cols", [P, 64])
        gru_b2, init_h, h0 = cols[:, 0:1], cols[:, 1:3], cols[:, 3:5]
        ln_g, ln_b, mlp_b2 = cols[:, 5:7], cols[:, 7:9], cols[:, 9:11]
        bias1, gate1 = cols[:, 11:12], cols[:, 12:13]
        eps, norm_bias, one = cols[:, 13:14], cols[:, 14:15], cols[:, 15:16]
        b1_raw, b1_eff = cols[:, 16:28].rearrange("p (l j) -> p l j", l=2), cols[:, 28:40].rearrange("p (l j) -> p l j", l=2)
        small = cols[:, 40:52]
        wqkv = sb("wqkv", [P, DEPTH, 3 * INNER])
        wo = sb("wo", [P, DEPTH, PAIRS, D])
        w1 = sb("w1", [P, DEPTH, 2 * HID])
        w2 = sb("w2", [P, DEPTH, JM, D])
        wqk1 = sb("wqk1", [P, 2, H1 * K1])
        wv1 = sb("wv1", [P, H1 * V1])
        wo1 = sb("wo1", [P, H1 // 2, D])
        xin = sb("xin", [P, NT, D])
        x_new, x0, xn0, xn1, x2, x3, gru_o = (
            sb(n, [P, N]) for n in ("x_new", "x0", "xn0", "xn1", "x2", "x3", "gru_o"))
        mlp_in, sq, cent, rstd = (sb(n, [P, N]) for n in ("mlp_in", "sq", "cent", "rstd"))
        mlp_h = sb("mlp_h", [P, JM, N])
        hsh = sb("hsh", [P, N])
        va, vb = sb("va", [P, NT, HEADS, DH + 1]), sb("vb", [P, NT, HEADS, DH + 1])
        qT, kT = sb("qT", [P, PAIRS, N]), sb("kT", [P, PAIRS, WIN + N])
        stat = sb("stat", [P, 112])
        scratch = sb("scratch", [P, 6144])
        sc = lambda at, n: scratch[:, at:at + n]
        l_sq, l_qk = sc(0, 1024), [sc(1024, 1024), sc(2048, 1024)]
        l_c, l_s, l_q = sc(3072, 1024), sc(4096, 1024), sc(5120, 1024)
        prob = [sc(512 * i, 512).rearrange("p (h n) -> p h n", n=P) for i in range(2)]
        probT = [sc(1024 + 512 * i, 512).rearrange("p (h n) -> p h n", n=P) for i in range(2)]
        o_row, oT = sc(2048, INNER), sc(2560, INNER).rearrange("p (r n) -> p r n", r=PAIRS)
        side = sb("side", [P, 7, N])
        g_c, g_f, g_i, g_m, g_r = (side[:, n, :] for n in range(5))
        g_fi, g_cfi = side[:, 1:3, :], side[:, 0:3, :]
        g_h = [side[:, 5 + j, :] for j in range(JG)]
        s_sig, s_g = side[:, 0, :], side[:, 1, :]
        parts = side[:, 0:3, :].rearrange("p a n -> p (a n)").bitcast(BF16).rearrange("p (c i n) -> p c i n", c=2, i=3)
        rest = [side[:, 3 + i, :] for i in range(2)]
        qs, ks = (sb(n, [STACK, 2, G1, N], BF16) for n in ("qs", "ks"))
        vrow = sb("vrow", [P, NT, H1 * V1])
        ex = sb("ex", [P, 2, 4, N])
        nmax, rsum, rinv = sb("nmax", [P, 8]), sb("rsum", [P, 2, 4]), sb("rinv", [P, 2, 4])
        vsc = sb("vsc", [P, 2, 4, V1])
        o1T = sb("o1T", [P, N])
        x1, gate, yf, yrow = (sb(n, [P, N])[:] for n in ("x1", "gate", "yf", "yrow"))
        store = nc.dram_tensor("parts_store", [B, 2, 2, len(Q_PART), K1, H1 // 2, N], BF16, kind="Internal").ap()

        pb = ctx.enter_context(nc.psum_tensor("pb", [P, 4, 512], F32))
        bank_a, bank_b, bank_c, bank_d = (pb[:, i, :] for i in range(4))

        def post0_bank(s):
            n = (("centre", 0), ("var", 0), ("g", 0), ("g", 1), ("g", 2), ("a", 0), ("a", 1), ("a", 2), ("y",)).index(s)
            return (bank_a, bank_b, bank_c)[n % 3]

        s_bank = [bank("s0"), bank("s1")]
        o_bank, y_bank = bank("o_bank"), bank("y_bank")

        token_rows = a["L0_attn_x"].rearrange("b (t p) d -> b p t d", p=P)
        out_rows = out.rearrange("b (t p) d -> b p t d", p=P)

        raw_masks = sc(0, 2 * P)
        base_tab = sc(2 * P, 2 * NT * 2 * DH).rearrange("p (c t k d) -> p c t k d", c=2, t=NT, k=2)
        raw_q, raw_k = ex[:, 0, 0, 0:256].rearrange("p (r d) -> p r d", r=2), ex[:, 0, 1, 0:256].rearrange("p (r d) -> p r d", r=2)
        raw_v = ex[:, 0, 2:4, :].rearrange("p a (r d) -> p (a r) d", d=D)
        raw_o = ex[:, 1, 0:2, :].rearrange("p a n -> p (a n)")
        qk_scale = ex[:, 1, 2, 0:4 * DH].rearrange("p (l k d) -> p l k d", l=2, k=2)
        ew = [ex[:, i, 0, :] for i in range(2)]
        ew2 = [ex[:, i, 1, :].rearrange("p (j d) -> p j d", j=JF) for i in range(2)]
        eh = sc(0, JF * N).rearrange("p (j n) -> p j n", j=JF)
        eacc = sc(2048, N).rearrange("p (t d) -> p t d", t=NT)
        ewt = sc(2560, E * NT).rearrange("p (e t) -> p e t", e=E)
        etmp = sc(2600, E * NT * TOPK).rearrange("p (e t k) -> p e t k", e=E, k=TOPK)
        ehf = sc(2700, NT * TOPK).rearrange("p (t k) -> p t k", k=TOPK)
        ews = sc(2720, NT * TOPK).rearrange("p (t k) -> p t k", k=TOPK)
        eidx = scratch[:, 2740:2740 + NT * TOPK].bitcast(I32).rearrange("p (t k) -> p t k", k=TOPK)
        es = [sc(3072 + N * i, N) for i in range(4)]
        col = lambda v: v.rearrange("(j p) -> p j", p=P)
        LOADS = [
            (const[:], a["const"][:, 0:3 * P]),
            (sc(0, 2 * P + 2 * NT * 2 * DH), a["const"][:, 3 * P:]),
            (gru_w1[:], a["L0_attn_W1"]),
            (gru_w2[:], a["L0_attn_W2"].rearrange("(j p) d -> p j d", p=P)),
            (wo[:], a["L0_ffn_wo"].rearrange("l (j p) d -> p l j d", p=P)),
            (wqkv[:], a["L0_ffn_wqkv"].rearrange("l p n -> p l n")),
            (w1[:], a["L0_ffn_w1"].rearrange("l p n -> p l n")),
            (raw_q, a["L1_attn_query_proj"].rearrange("h k d -> (h k) d").rearrange("(r p) d -> p r d", p=P)),
            (raw_k, a["L1_attn_key_proj"].rearrange("h k d -> (h k) d").rearrange("(r p) d -> p r d", p=P)),
            (raw_v, a["L1_attn_value_proj"].rearrange("h k d -> (h k) d").rearrange("(r p) d -> p r d", p=P)),
            (raw_o, a["L1_attn_output_proj"].rearrange("d h v -> d (h v)")),
            (gru_b2, col(a["L0_attn_b2"])),
            (init_h, col(a["L0_attn_init_h"])),
            (bias1, col(a["L1_ffn_bias"])),
            (ln_g, a["L0_ffn_ln_g"].rearrange("l p -> p l")),
            (ln_b, a["L0_ffn_ln_b"].rearrange("l p -> p l")),
            (mlp_b2, a["L0_ffn_b2"].rearrange("l p -> p l")),
        ]
        for l in range(DEPTH):
            LOADS += [
                (w2[:, l, 0:2, :], a["L0_ffn_w2"][l, 0:2 * P, :].rearrange("(j p) d -> p j d", p=P)),
                (w2[0:ROWS[2], l, 2, :], a["L0_ffn_w2"][l, 2 * P:HID, :]),
                (qk_scale[:, l, 0, :], a["L0_ffn_q_scale"][l:l + 1, :].to_broadcast([P, DH])),
                (qk_scale[:, l, 1, :], a["L0_ffn_k_scale"][l:l + 1, :].to_broadcast([P, DH])),
            ]
            for g in range(2):
                LOADS += [
                    (b1_raw[:, l, 3 * g:3 * g + 2], col(a["L0_ffn_b1"][l, g * HID:g * HID + 2 * P])),
                    (b1_raw[0:ROWS[2], l, 3 * g + 2:3 * g + 3],
                     a["L0_ffn_b1"][l, g * HID + 2 * P:(g + 1) * HID].rearrange("(p o) -> p o", o=1)),
                ]
        for k in range(3):
            LOADS += [(gru_b1[:, k, :], col(a["L0_attn_b1"][k * DIN:(k + 1) * DIN]))]
        N_LOADS = 16 * len(LOADS)

        block = ctx.enter_context(nc.Block())

        @block.sync
        def _(sp):
            for dst, src in LOADS:
                sp.dma_start(dst, src).then_inc(loaded, 16)

            def load_x(b):
                need(sp, pre, "pe", b - 1, ("x",), "x")
                sp.dma_start(xin[:], token_rows[b]).then_inc(x_loaded, 16)

            def store_parts(b):
                for c in range(4):
                    need(sp, post[1], "dve", b, ("qk2", c), "p2")
                    for slot, part, n, times in (K_STORES if c >= 2 else Q_STORES):
                        src = parts[:, c % 2, part:part + n, :]
                        if times > 1:
                            src = src.broadcast_to([P, times, N])
                        dst = store[b, c // 2, c % 2, slot:slot + n * times].rearrange("i k h n -> (k h) i n")
                        sp.dma_start(dst, src).then_inc(parts_stored[c % 2], 16)

            def load_stack(b, g):
                if g < 2:
                    need(sp, glob, "pe", b - 1, ("sim", G1 * (g + GROUPS - 2) + G1 - 1, 3), "s")
                else:
                    need(sp, glob, "pe", b, ("sim", G1 * (g - 2) + G1 - 1, 3), "s")
                if g == 0:
                    for p in parts_stored:
                        sp.wait_ge(p, b * (2 * PUT_COUNT) + 2 * PUT_COUNT)
                half, h = divmod(G1 * g, H1 // 2)
                for dst, which in ((qs, 0), (ks, 1)):
                    sp.dma_start(dst[:, g % 2, :, :], store[b, which, half, :, :, h:h + G1, :].rearrange("i k h n -> (i k) h n"))\
                        .then_inc(stack_loaded[g % 2], 16)

            def store_out(b):
                need(sp, glob, "act", b, ("store",), "t")
                sp.dma_start(out_rows[b], yrow[:].rearrange("p (t d) -> p t d", t=NT)).then_inc(out_stored, 16)

            def load_experts():
                for e in range(E):
                    if e >= 2:
                        sp.wait_ge(expert_pe, 8 * (e - 1))
                    else:
                        sp.wait_ge(prep_pe, 1)
                        sp.wait_ge(prep_dve, 1)
                    sp.dma_start(ew[e % 2], a["L1_ffn_w1"][e]).then_inc(expert_loaded, 16)
                    sp.dma_start(ew2[e % 2], a["L1_ffn_w2"][e].rearrange("(j p) d -> p j d", p=P)).then_inc(expert_loaded, 16)
                    sp.wait_ge(expert_loaded, 32 * (e + 1))

            def step(i):
                has = lambda b: not isinstance(i, int) or 0 <= b < B
                if has(i + 1):
                    load_x(i + 1)
                if has(i - 2):
                    load_stack(i - 2, 6)
                    load_stack(i - 2, 7)
                if has(i - 1):
                    store_parts(i - 1)
                    load_stack(i - 1, 0)
                    load_stack(i - 1, 1)
                if has(i - 2):
                    store_out(i - 2)
                if isinstance(i, int) and i == 1:
                    load_experts()
                if has(i - 1):
                    for g in range(2, 6):
                        load_stack(i - 1, g)

            load_x(0)
            step(0)
            step(1)
            with sp.Fori(2, B - 1) as i:
                step(i)
            for i in range(B - 1, B + 2):
                step(i)
            sp.wait_ge(out_stored, 16 * B + 16)
            for p in parts_stored:
                sp.wait_ge(p, 2 * PUT_COUNT * B)

        def run(eng, name, does, expert):
            for f in flows.values():
                if name in f.sem:
                    eng.sem_inc(f.sem[name], f.per[name])

            def steps(i, order):
                n, loop_i = 0, i
                for flow, shift, s in order:
                    if name not in MARKS[flow][s[0]]:
                        continue
                    if not isinstance(i, int) and n % FRESH == 0:
                        copy = eng.alloc_register(f"step_{n}")
                        eng.reg_mov(copy, loop_i)
                        i = eng.snap(copy, donate=True, min_val=2, max_val=B - 2)
                    n += 1
                    if not isinstance(i, int) or 0 <= i + shift < B:
                        b = i + shift if shift > 0 else i - -shift if shift else i
                        does[flow](b, s)

            steps(-1, merged(name))
            steps(0, merged(name))
            early = lambda x: x[0] in ("attn0", "post1", "keep0", "keep1") or x[2][0] == "values"
            steps(1, [x for x in merged(name) if early(x)])
            expert()
            steps(1, [x for x in merged(name) if not early(x)])
            with eng.Fori(2, B - 1) as i:
                if name == "act":
                    eng.preload_act_table_set(EXP_LN)
                steps(i, merged(name))
            for i in range(B - 1, B + 2):
                steps(i, merged(name))

        @block.tensor
        def _(pe):
            def mm(o, l, r, start=True, stop=True):
                return pe.matmul(o, l, r, start=start, stop=stop, skip_group_check=True)

            pe.wait_ge(loaded, N_LOADS)
            for r in range(2):
                pe.transpose(pb[:, 0, P * r:P * r + P], raw_q[:, r, :], ident)
                pe.transpose(pb[:, 1, P * r:P * r + P], raw_k[:, r, :], ident)
            for r in range(8):
                pe.transpose(pb[:, 2 + r // 4, P * (r % 4):P * (r % 4) + P], raw_v[:, r, :], ident)
            for r in range(8):
                pe.transpose(s_bank[r // 4][:, P * (r % 4):P * (r % 4) + P], raw_o[:, P * r:P * r + P], ident)
            for l in range(DEPTH):
                for g in range(2):
                    for j in range(JM):
                        i = 6 * l + 3 * g + j
                        last = mm(o_bank[0:ROWS[j], i:i + 1], w1[:, l, g * HID + P * j:g * HID + P * j + ROWS[j]],
                                  ln_b[:, l:l + 1])
            last.then_inc(prep_pe, 1)
            pe.wait_ge(prep_dve, 2)
            pe.wait_ge(prep_act, 1)
            pe.wait_ge(prep_pool, 1)

            def norm(f, b, s, src):
                dst = post0_bank(s) if f is post[0] else bank_d
                if s[0] == "centre":
                    mm(dst, centre, src).then_inc(f.sem["pe"], 1)
                else:
                    need(pe, f, "act", b, ("centre", s[1]), "sq")
                    mm(dst, mean, sq[:]).then_inc(f.sem["pe"], 1)

            def pre_does(b, s):
                if s[0] == "x":
                    pe.wait_ge(x_loaded, b * 16 + 16)
                    need(pe, gru, "act", b - 1, ("out",), "o")
                    for t in range(NT):
                        last = pe.transpose(bank_d[:, P * t:P * t + P], xin[:, t, :], ident)
                    last.then_inc(pre.sem["pe"], 1)
                else:
                    if s[0] == "centre":
                        need(pe, pre, "act", b, ("x",), "x")
                    norm(pre, b, s, x_new[:])

            def gru_does(b, s):
                kind = s[0]
                if kind == "out":
                    need(pe, gru, "dve", b, ("g5", 1), "h")
                    mm(bank_d, gru_w2[:, 0, :], g_h[0], stop=False)
                    mm(bank_d, gru_w2[:, 1, :], g_h[1], start=False).then_inc(gru.sem["pe"], 1)
                    return
                j, k = s[1], ("in_h", "in_f", "in_i").index(kind)
                if k:
                    need(pe, gru, "dve", b, *((("in_h", j), "r") if k == 1 else (("in_f", j), "f")))
                elif j:
                    need(pe, gru, "dve", b, ("in_i", j - 1), "i")
                else:
                    need(pe, post[1], "dve", b - 1, ("qk", 3), "r")
                    need(pe, post[0], "dve", b, ("y",), "x")
                mm(bank_d, gru_w1[:, k * DIN + P * j:k * DIN + P * j + P], xn0[:]).then_inc(gru.sem["pe"], 1)

            def attn_does(l, b, s):
                f, kind = attn[l], s[0]
                if kind in ("q", "k", "v"):
                    t = s[1]
                    if l and t == 0:
                        need(pe, post[0], "dve", b, *{"q": (("a", 1), "a"), "k": (("a", 2), "a"), "v": (("y",), "x")}[kind])
                        if kind == "q":
                            need(pe, f, "dve", b, ("shift",), "h")
                    elif kind == "v":
                        if t:
                            need(pe, f, "dve", b, ("v", t - 1), "c")
                        else:
                            need(pe, attn[1], "dve", b - 1, ("wo", NT - 1), "x")
                    elif t >= 2:
                        need(pe, f, "act", b, ("t" + kind, t - 2), "t")
                    elif t:
                        need(pe, f, "act", b, (kind, 0), "c")
                    elif kind == "q":
                        need(pe, attn[1], "dve", b - 1, ("score", 2 * NT - 1), "sub")
                        need(pe, f, "dve", b, ("shift",), "h")
                    else:
                        need(pe, attn[1], "act", b - 1, ("oturn", NT - 1), "t")
                    n = ("q", "k", "v").index(kind)
                    mm((bank_a, bank_b, bank_c)[n], hsh[:, P * t:P * t + P], wqkv[:, l, INNER * n:INNER * (n + 1)])\
                        .then_inc(f.sem["pe"], 1)
                elif kind in ("tq", "tk"):
                    t, k = s[1], int(kind == "tk")
                    dst = (bank_a, bank_b)[k] if t < NT - 1 else (bank_b, bank_c)[k]
                    if t < NT - 1:
                        need(pe, f, "act", b, (kind[1], t + 1), "c")
                    else:
                        need(pe, f, *(("dve", b, ("v", t), "c") if k else ("act", b, ("tk", t - 1), "t")))
                    need(pe, f, "pool", b, ("rot2", t), "q")
                    for r in range(PAIRS):
                        last = pe.transpose(dst[:, P * r:P * r + P],
                                            l_q[:, INNER * k + P * r:INNER * k + P * r + P], ident)
                    last.then_inc(f.sem["pe"], 1)
                elif kind == "score":
                    t, par = s[1] // 2, s[1] % 2
                    if s[1]:
                        need(pe, f, "dve", b, ("score", s[1] - 1), "sub")
                    else:
                        need(pe, f, "act", b, ("tq", NT - 2), "t")
                    need(pe, f, "act", b, ("tk", t), "t")
                    mm(bank_a, identb[:], masks[:, 0 if t == 0 else 1, :, :].rearrange("p h n -> p (h n)"), stop=False)
                    for r in range(PAIRS):
                        rows, at = slice(DH * par, DH * par + DH), P * t
                        for c, k in ((0, at + WIN), (WIN, at)):
                            mm(bank_a[0:WIN, P * r + c:P * r + c + WIN], qT[rows, r, at:at + WIN], kT[rows, r, k:k + WIN],
                               start=False)
                        last = mm(bank_a[WIN:P, P * r:P * r + P], qT[rows, r, at + WIN:at + P],
                                  kT[rows, r, at + WIN:at + WIN + P], start=False)
                    last.then_inc(f.sem["pe"], 1)
                elif kind == "pturn":
                    u = s[1]
                    if u == 0:
                        need(pe, f, "act", b, ("tq", NT - 1), "t")
                    elif u >= 4 and u % 2 == 0:
                        need(pe, f, "act", b, ("oturn", u // 2 - 2), "t")
                    else:
                        need(pe, f, "act", b, ("pturn", u - 1), "t")
                    need(pe, f, "act", b, ("prob", u), "p")
                    for r in range(PAIRS):
                        last = pe.transpose(bank_b[:, P * r:P * r + P], prob[u % 2][:, r, :], ident)
                    last.then_inc(f.sem["pe"], 1)
                elif kind == "pv":
                    u = s[1]
                    t, par = u // 2, u % 2
                    if u == 0:
                        need(pe, f, "act", b, ("tk", NT - 1), "t")
                    elif u >= 3 and u % 2 == 1:
                        need(pe, f, "dve", b, ("wo", (u + 1) // 2 - 2), "x")
                    else:
                        need(pe, f, "dve", b, ("pv", u - 1), "o")
                    need(pe, f, "act", b, ("pturn", u), "t")
                    for r in range(PAIRS):
                        for w, v in ((0, vb), (1, va)):
                            last = mm(bank_c[WIN * w:WIN * w + WIN, (DH + 1) * r:(DH + 1) * (r + 1)],
                                      probT[u % 2][:, r, WIN * w:WIN * w + WIN], v[:, t, 2 * r + par, :])
                    last.then_inc(f.sem["pe"], 1)
                elif kind == "oturn":
                    t = s[1]
                    need(pe, f, "act", b, *((("pturn", 2 * t + 3), "t") if t < NT - 1 else (("oturn", t - 1), "t")))
                    need(pe, f, "dve", b, ("pv", 2 * t + 1), "o")
                    for r in range(PAIRS):
                        last = pe.transpose(bank_b[:, P * r:P * r + P], o_row[:, P * r:P * r + P], ident)
                    last.then_inc(f.sem["pe"], 1)
                elif kind == "wo":
                    t = s[1]
                    need(pe, f, "dve", b, ("pv", min(2 * t + 2, 2 * NT - 1)), "o")
                    need(pe, f, "act", b, ("oturn", t), "t")
                    for r in range(PAIRS):
                        last = mm(bank_c[:, 0:P], wo[:, l, r, :], oT[:, r, :], start=(r == 0), stop=(r == PAIRS - 1))
                    last.then_inc(f.sem["pe"], 1)

            def post_does(l, b, s):
                f, kind = post[l], s[0]
                if kind == "centre":
                    if s[1] == "out":
                        need(pe, f, "pool", b, ("silu3",), "x")
                    else:
                        if l == 0:
                            need(pe, attn[0], "dve", b, ("score", 2 * NT - 1), "sub")
                        elif isinstance(b, int) and b == B - 1:
                            need(pe, gru, "act", b, ("out",), "o")
                        else:
                            need(pe, pre, "dve", b + 1, ("rstd", "in"), "n2")
                        need(pe, f, "dve", b, ("shift",), "h")
                    norm(f, b, s, x3[:] if s[1] == "out" else mlp_in[:])
                elif kind == "var":
                    if l == 0:
                        need(pe, attn[0], "act", b, ("oturn", NT - 1), "t")
                    norm(f, b, s, None)
                elif kind in ("g", "a"):
                    j = s[1]
                    if l == 0:
                        if kind == "a":
                            need(pe, f, "act", b, ("g", j), "g")
                        elif j == 0:
                            need(pe, attn[0], "dve", b, ("wo", NT - 1), "x")
                        if kind == "g":
                            need(pe, f, "dve", b, ("normed", l), "n")
                    elif kind == "g":
                        need(pe, f, *(("act", b, ("g", j - 1), "g") if j else ("dve", b, ("normed", l), "n")))
                    else:
                        need(pe, f, *(("dve", b, ("a", j - 1), "a") if j else ("act", b, ("g", JM - 1), "g")))
                    at = HID * (kind == "g") + P * j
                    dst = bank_d if l else post0_bank(s)
                    mm(dst[0:ROWS[j], :], w1[:, l, at:at + ROWS[j]], cent[:]).then_inc(f.sem["pe"], 1)
                elif kind == "y":
                    need(pe, f, "dve", b, ("a", JM - 1), "a")
                    dst = bank_d if l else post0_bank(s)
                    for j in range(JM):
                        last = mm(dst, w2[0:ROWS[j], l, j, :], mlp_h[0:ROWS[j], j, :], start=(j == 0), stop=(j == JM - 1))
                    last.then_inc(f.sem["pe"], 1)
                elif kind == "qk":
                    c = s[1]
                    need(pe, f, *(("dve", b, ("qk", c - 1), "r") if c else ("dve", b, ("normed", "out"), "n")))
                    mm(bank_d, wqk1[:, c // 2, P * (c % 2):P * (c % 2) + P], xn1[:]).then_inc(f.sem["pe"], 1)

            def glob_does(b, s):
                kind, GE = s[0], glob.sem["pe"]
                if kind == "values":
                    n = s[1]
                    if n >= 2:
                        need(pe, glob, "act", b, ("values", n - 2), "v")
                    else:
                        need(pe, glob, "act", b - 1, ("sim", H1 - 1, 2 + n), "e")
                    if n == 0:
                        need(pe, post[1], "dve", b, ("normed", "out"), "n")
                    mm(s_bank[n % 2][:], xn1[:, P * (n // 2):P * (n // 2) + P], wv1[:, 512 * (n % 2):512 * (n % 2) + 512])\
                        .then_inc(GE, 1)
                elif kind == "sim":
                    _, h, m = s
                    c = 4 * h + m
                    g = h // G1
                    if m == 0 and h % G1 == 0:
                        pe.wait_ge(stack_loaded[g % 2], (b * (GROUPS // 2) + g // 2 + 1) * STACK_COUNT)
                    if c >= 2:
                        need(pe, glob, "act", b, ("sim", (c - 2) // 4, (c - 2) % 4), "e")
                    else:
                        need(pe, glob, "act", b, ("values", 2 * NT - 2 + c), "v")
                    mm(s_bank[c % 2][:], ks[:, g % 2, h % G1, P * m:P * m + P], qs[:, g % 2, h % G1, :]).then_inc(GE, 1)
                elif kind == "av":
                    h = s[1]
                    need(pe, glob, "pool", b, ("scale_v", h), "v")
                    if h % 2 == 0:
                        if h:
                            need(pe, glob, "act", b, ("o", h // 2 - 1), "t")
                        else:
                            need(pe, glob, "act", b - 1, ("o", 7), "t")
                    for m in range(4):
                        last = mm(o_bank[V1 * (h % 2):V1 * (h % 2) + V1, :], vsc[:, h % 2, m, :], ex[:, h % 2, m, :],
                                  start=(m == 0), stop=(m == 3))
                    last.then_inc(GE, 1)
                elif kind == "proj":
                    p = s[1]
                    need(pe, glob, "act", b, ("o", p), "t")
                    if p == 0:
                        need(pe, glob, "act", b - 1, ("store",), "t")
                    mm(y_bank[:], wo1[:, p, :], o1T[:], start=(p == 0), stop=(p == 7)).then_inc(GE, 1)
                elif kind == "store":
                    need(pe, glob, "pool", b, ("gate",), "x")
                    for t in range(NT):
                        last = pe.transpose(y_bank[:, P * t:P * t + P], yf[:, P * t:P * t + P], ident)
                    last.then_inc(GE, 1)

            def expert():
                need(pe, attn[0], "dve", 1, ("wo", NT - 1), "x")
                need(pe, post[1], "dve", 0, ("qk", 3), "r")
                need(pe, glob, "act", 0, ("values", 2 * NT - 1), "v")
                n = 0
                for e in range(E):
                    pe.wait_ge(expert_loaded, 32 * (e + 1))
                    for j in range(JF):
                        if e:
                            pe.wait_ge(expert_act, JF * (e - 1) + j + 1)
                        mm(pb[:, j, :], ew[e % 2][:, P * j:P * j + P], xn1[:]).then_inc(expert_pe, 1)
                    for t in range(NT):
                        if t == 0:
                            pe.wait_ge(expert_act, JF * (e + 1))
                        if n >= 2:
                            pe.wait_ge(expert_dve, n - 1)
                        for j in range(JF):
                            last = mm(s_bank[n % 2][:, 0:P], eh[:, j, P * t:P * t + P], ew2[e % 2][:, j, :],
                                      start=(j == 0), stop=(j == JF - 1))
                        last.then_inc(expert_pe, 1)
                        n += 1
                pe.wait_ge(expert_dve, n)
                for t in range(NT):
                    last = pe.transpose(y_bank[:, P * t:P * t + P], eacc[:, t, :], ident)
                last.then_inc(expert_pe, 1)
                pe.wait_ge(expert_dve, n + 1)

            run(pe, "pe", {
                "pre": pre_does, "gru": gru_does, "glob": glob_does,
                "attn0": lambda b, s: attn_does(0, b, s), "attn1": lambda b, s: attn_does(1, b, s),
                "post0": lambda b, s: post_does(0, b, s), "post1": lambda b, s: post_does(1, b, s)}, expert)

        @block.scalar
        def _(act):
            A = nc.scalar.activation
            act.sem_inc(out_stored, 16)
            act.preload_act_table_set(EXP_LN)
            act.wait_ge(prep_pe, 1)
            nc.scalar.activation(wv1[:].rearrange("p (a n) -> p a n", a=2), pb[:, 2:4, :], ACT.Copy)
            for i in range(2):
                last = nc.scalar.activation(wo1[:, 4 * i:4 * i + 4, :].rearrange("p r d -> p (r d)"), s_bank[i][:], ACT.Copy)
            act.wait_ge(prep_dve, 1)
            A(small[:, 3:6], small[:, 0:3], ACT.Exp).then_inc(prep_act, 1)
            act.wait_ge(prep_act, 1)
            A(small[:, 6:9], small[:, 3:6], ACT.Ln, bias=1.0).then_inc(prep_act, 1)
            act.wait_ge(prep_dve, 3)
            A(small[:, 0:3], small[:, 9:12], ACT.Exp).then_inc(prep_act, 1)

            def norm(f, b, s):
                FA, k = f.sem["act"], s[1]
                if s[0] == "centre":
                    need(act, f, "dve", b, s, "c")
                    A(sq[:], cent[:], ACT.Square).then_inc(FA, 1)
                elif s[0] == "var":
                    need(act, f, "pe", b, s, "v")
                    A(rstd[:], post0_bank(s) if f is post[0] else bank_d, ACT.Ln, bias=eps).then_inc(FA, 1)
                else:
                    need(act, f, "act", b, ("var", k), "ln")
                    A(rstd[:], rstd[:], ACT.Exp, scale=-0.5).then_inc(FA, 1)

            def pre_does(b, s):
                if s[0] == "x":
                    need(act, pre, "pe", b, s, "x")
                    need(act, keep0, "pool", b - 1, ("x0",), "c")
                    A(x_new[:], bank_d, ACT.Copy).then_inc(pre.sem["act"], 1)
                else:
                    norm(pre, b, s)

            def gru_does(b, s):
                kind, GA = s[0], gru.sem["act"]
                if kind == "g2":
                    need(act, gru, "pool", b, ("g1", s[1]), "i")
                    A(g_cfi, g_cfi, ACT.Exp).then_inc(GA, 1)
                    need(act, gru, "dve", b, ("in_h", s[1]), "m")
                    A(sq[:], g_m, ACT.Exp).then_inc(GA, 1)
                    need(act, gru, "act", b, s, "m")
                    A(sq[:], sq[:], ACT.Ln, bias=1.0).then_inc(GA, 1)
                elif kind == "g3":
                    need(act, gru, "dve", b, ("g2", s[1]), "d")
                    A(g_c, g_c, ACT.Ln).then_inc(GA, 1)
                    need(act, gru, "act", b, s, "ld")
                    A(g_c, g_c, ACT.Exp, scale=-1.0).then_inc(GA, 1)
                elif kind == "g4":
                    need(act, gru, "pool", b, ("g3", s[1]), "t")
                    A(g_m, g_m, ACT.Exp).then_inc(GA, 1)
                elif kind == "out":
                    need(act, gru, "pe", b, s, "o")
                    need(act, post[1], "pool", b - 1, ("silu3",), "g")
                    A(gru_o[:], bank_d, ACT.Identity, bias=gru_b2).then_inc(GA, 1)

            def attn_does(l, b, s):
                f, kind = attn[l], s[0]
                FA = f.sem["act"]
                if kind in ("q", "k"):
                    t, k = s[1], int(kind == "k")
                    src = bank_b if k else bank_a
                    need(act, f, "pe", b, s, "p")
                    if t:
                        need(act, f, "dve", b, ("rot", t - 1), "ss")
                    A(l_sq[:, INNER * k:INNER * (k + 1)], src, ACT.Square).then_inc(FA, 1)
                    if t >= 2:
                        need(act, f, "dve", b, ("rot", t - 2), "s1")
                    A(l_qk[t % 2][:, INNER * k:INNER * (k + 1)], src, ACT.Copy).then_inc(FA, 1)
                elif kind == "vb":
                    t = s[1]
                    need(act, f, "dve", b, ("v", t), "c")
                    if t < NT - 1:
                        A(vb[WIN:P, t + 1, :, 0:DH], va[WIN:P, t, :, 0:DH], ACT.Copy)
                    A(vb[0:WIN, t, :, 0:DH], va[0:WIN, t, :, 0:DH], ACT.Copy).then_inc(FA, 1)
                elif kind == "rot":
                    need(act, f, "dve", b, s, "max")
                    A(stat[:, 16:32], stat[:, 0:16], ACT.Ln, scale=2.0 ** NORM_SHIFT).then_inc(FA, 1)
                    need(act, f, "act", b, s, "ln")
                    A(stat[:, 32:48], stat[:, 16:32], ACT.Exp, scale=-0.5, bias=norm_bias).then_inc(FA, 1)
                elif kind in ("tq", "tk"):
                    t = s[1]
                    need(act, f, "pe", b, s, "t")
                    if kind == "tq":
                        dst, src = qT[:, :, P * t:P * t + P], bank_a if t < NT - 1 else bank_b
                    else:
                        dst, src = kT[:, :, WIN + P * t:WIN + P * t + P], bank_b if t < NT - 1 else bank_c
                    A(dst, src.rearrange("p (r n) -> p r n", r=PAIRS), ACT.Copy).then_inc(FA, 1)
                elif kind == "prob":
                    need(act, f, "dve", b, ("score", s[1]), "sub")
                    A(prob[s[1] % 2], prob[s[1] % 2], ACT.Exp).then_inc(FA, 1)
                elif kind == "pturn":
                    u = s[1]
                    need(act, f, "pe", b, s, "t")
                    if u >= 2:
                        need(act, f, "pe", b, ("pv", u - 2), "o")
                    A(probT[u % 2], bank_b.rearrange("p (r n) -> p r n", r=PAIRS), ACT.Copy).then_inc(FA, 1)
                elif kind == "oturn":
                    need(act, f, "pe", b, s, "t")
                    A(oT, bank_b.rearrange("p (r n) -> p r n", r=PAIRS), ACT.Copy).then_inc(FA, 1)

            def post_does(l, b, s):
                f, kind = post[l], s[0]
                FA = f.sem["act"]
                if kind in ("centre", "var", "rstd"):
                    norm(f, b, s)
                elif kind == "g":
                    j = s[1]
                    r = ROWS[j]
                    need(act, f, "pe", b, s, "p")
                    A(mlp_h[0:r, j, :], (bank_d if l else post0_bank(s))[0:r, :], ACT.Identity, bias=b1_eff[0:r, l, 3 + j:4 + j]).then_inc(FA, 1)
                elif kind == "gelu":
                    need(act, f, "act", b, ("g", JM - 1), "g")
                    A(mlp_h[:, 0:2, :], mlp_h[:, 0:2, :], ACT.Gelu)
                    A(mlp_h[0:ROWS[2], 2, :], mlp_h[0:ROWS[2], 2, :], ACT.Gelu).then_inc(FA, 1)
                    act.preload_act_table_set(EXP_LN)
                elif kind == "silu1":
                    need(act, f, "dve", b, s, "a")
                    A(s_sig, s_sig, ACT.Exp).then_inc(FA, 1)
                    need(act, f, "act", b, s, "e")
                    A(s_sig, s_sig, ACT.Ln, bias=1.0).then_inc(FA, 1)
                elif kind == "silu2":
                    need(act, f, "dve", b, s, "d")
                    A(s_sig, s_sig, ACT.Exp).then_inc(FA, 1)
                elif kind == "qk":
                    c = s[1]
                    need(act, f, "pe", b, s, "p")
                    if c >= 2:
                        act.wait_ge(parts_stored[c % 2], b * (2 * PUT_COUNT) + PUT_COUNT)
                    scale = K1 ** -0.5 if c < 2 else 1.0
                    A(parts[:, c % 2, 0, :], bank_d, ACT.Copy, scale=scale).then_inc(FA, 1)
                elif kind == "qk2":
                    c = s[1]
                    need(act, f, "dve", b, ("qk", c), "r")
                    A(parts[:, c % 2, 1, :], rest[c % 2], ACT.Copy).then_inc(FA, 1)

            def glob_does(b, s):
                kind, GA = s[0], glob.sem["act"]
                if kind == "values":
                    n = s[1]
                    need(act, glob, "pe", b, s, "p")
                    if n == 0:
                        need(act, glob, "pool", b - 1, ("scale_v", H1 - 1), "v")
                    A(vrow[:, n // 2, 512 * (n % 2):512 * (n % 2) + 512], s_bank[n % 2][:], ACT.Copy).then_inc(GA, 1)
                elif kind == "sim":
                    _, h, m = s
                    c = 4 * h + m
                    need(act, glob, "dve", b, s, "max")
                    if m == 0:
                        if h >= 2:
                            need(act, glob, "pe", b, ("av", h - 2), "o")
                        else:
                            need(act, glob, "pe", b - 1, ("av", H1 - 2 + h), "o")
                    A(ex[:, h % 2, m, :], s_bank[c % 2][:], ACT.Exp, bias=nmax[:, c % 8:c % 8 + 1],
                      accum_out=rsum[:, h % 2, m:m + 1]).then_inc(GA, 1)
                elif kind == "o":
                    p = s[1]
                    need(act, glob, "pe", b, ("av", 2 * p + 1), "o")
                    if p:
                        need(act, glob, "pe", b, ("proj", p - 1), "y")
                    A(o1T[:], o_bank[:], ACT.Copy).then_inc(GA, 1)
                elif kind == "store":
                    need(act, glob, "pe", b, s, "t")
                    act.wait_ge(out_stored, b * 16 + 16)
                    A(yrow[:], y_bank[:], ACT.Copy).then_inc(GA, 1)

            def expert():
                for e in range(E):
                    for j in range(JF):
                        act.wait_ge(expert_pe, 8 * e + j + 1)
                        if e:
                            act.wait_ge(expert_pe, 8 * e)
                        A(eh[:, j, :], pb[:, j, :], ACT.Gelu).then_inc(expert_act, 1)
                act.preload_act_table_set(EXP_LN)
                act.wait_ge(expert_dve, E * NT + 2)
                A(es[2], es[1], ACT.Exp).then_inc(expert_act, 1)
                act.wait_ge(expert_act, E * JF + 1)
                A(es[2], es[2], ACT.Ln, bias=1.0).then_inc(expert_act, 1)
                act.wait_ge(expert_dve, E * NT + 3)
                A(es[3], es[3], ACT.Exp).then_inc(expert_act, 1)

            run(act, "act", {
                "pre": pre_does, "gru": gru_does, "glob": glob_does,
                "attn0": lambda b, s: attn_does(0, b, s), "attn1": lambda b, s: attn_does(1, b, s),
                "post0": lambda b, s: post_does(0, b, s), "post1": lambda b, s: post_does(1, b, s)}, expert)

        @block.vector
        def _(dve):
            V = nc.vector
            dve.wait_ge(loaded, N_LOADS)
            dve.wait_ge(prep_pool, 1)
            V.tensor_copy(identb[:], ident)
            for i in range(2):
                for h in range(4):
                    V.tensor_copy(masks[:, i, h, :], raw_masks[:, i * P:(i + 1) * P])
            H = DH // 2
            for l in range(DEPTH):
                for k in range(2):
                    scl = qk_scale[:, l, k, :].unsqueeze(1).broadcast_to([P, NT, DH])
                    V.tensor_tensor(tab[:, l, 0, :, k, :], base_tab[:, 0, :, k, :], scl, ALU.mult)
                    V.tensor_tensor(tab[:, l, 1, :, k, 0:H], base_tab[:, 1, :, k, 0:H], scl[:, :, H:], ALU.mult)
                    V.tensor_tensor(tab[:, l, 1, :, k, H:], base_tab[:, 1, :, k, H:], scl[:, :, 0:H], ALU.mult)
            V.tensor_scalar(small[:, 0:2], init_h, 0.0, None, ALU.min)
            V.scalar_tensor_tensor(small[:, 2:3], bias1, -1.0, bias1, ALU.mult, ALU.min)
            V.tensor_scalar(h0, init_h, 0.0, None, ALU.max).then_inc(prep_dve, 1)
            dve.wait_ge(prep_pe, 1)
            for f in range(2):
                q, k = (wqk1[:, i, P * f:P * f + P].rearrange("p (k h) -> p k h", k=K1) for i in range(2))
                V.tensor_copy(q, pb[:, 0, 0:2 * P].rearrange("p (k f h) -> p f k h", k=K1, f=2)[:, f])
                V.tensor_copy(k, pb[:, 1, 0:2 * P].rearrange("p (f h k) -> p f k h", k=K1, f=2)[:, f])
            for l in range(DEPTH):
                for g in range(2):
                    for j in range(JM):
                        i = 3 * g + j
                        V.tensor_tensor(b1_eff[0:ROWS[j], l, i:i + 1], o_bank[0:ROWS[j], 6 * l + i:6 * l + i + 1],
                                        b1_raw[0:ROWS[j], l, i:i + 1], ALU.add)
                last = V.tensor_scalar(w1[:, l, :], w1[:, l, :], ln_g[:, l:l + 1], None, ALU.mult)
            last.then_inc(prep_dve, 1)
            dve.wait_ge(prep_act, 2)
            dve.wait_ge(prep_dve, 2)
            V.tensor_tensor(small[:, 9:11], small[:, 0:2], small[:, 6:8], ALU.subtract)
            V.scalar_tensor_tensor(small[:, 11:12], bias1, 0.0, small[:, 8:9], ALU.min, ALU.subtract).then_inc(prep_dve, 1)
            dve.wait_ge(prep_act, 3)
            V.tensor_tensor(h0, h0, small[:, 0:2], ALU.add)
            V.tensor_tensor(gate1, bias1, small[:, 2:3], ALU.mult).then_inc(prep_dve, 1)

            def norm(f, b, s, dst):
                FV, k = f.sem["dve"], s[1]
                if s[0] == "centre":
                    need(dve, f, "pe", b, s, "c")
                    if f is post[0]:
                        need(dve, post[1], "dve", b - 1, ("normed", "out"), "n")
                    V.tensor_copy(cent[:], post0_bank(s) if f is post[0] else bank_d).then_inc(FV, 1)
                elif s[0] == "rstd":
                    need(dve, f, "act", b, s, "r")
                    V.tensor_tensor(sq[:], rstd[:], rstd[:], ALU.mult).then_inc(FV, 1)
                    need(dve, f, "dve", b, s, "n1")
                    src = post0_bank(("var", k)) if f is post[0] else bank_d
                    V.scalar_tensor_tensor(sq[:], src, EPS, sq[:], ALU.add, ALU.mult).then_inc(FV, 1)
                else:
                    need(dve, f, "dve", b, ("rstd", k), "n2")
                    V.scalar_tensor_tensor(sq[:], sq[:], -3.0, rstd[:], ALU.add, ALU.mult).then_inc(FV, 1)
                    need(dve, f, "dve", b, s, "r")
                    V.scalar_tensor_tensor(dst, sq[:], -0.5, cent[:], ALU.mult, ALU.mult).then_inc(FV, 1)

            def pre_does(b, s):
                norm(pre, b, s, xn0[:])

            def gru_does(b, s):
                kind, j, GV = s[0], s[1], gru.sem["dve"]
                if kind == "in_h":
                    need(dve, gru, "pe", b, s, "p")
                    bh = gru_b1[:, 0, j:j + 1]
                    if j == 0:
                        need(dve, post[1], "dve", b - 1, ("qk2", 3), "p2")
                    else:
                        need(dve, gru, "dve", b, ("g5", j - 1), "h")
                    V.tensor_scalar(g_m, bank_d, bh, 0.0, ALU.add, ALU.min).then_inc(GV, 1)
                    V.tensor_scalar(g_r, bank_d, bh, 0.0, ALU.add, ALU.max).then_inc(GV, 1)
                elif kind == "in_f":
                    need(dve, gru, "pe", b, s, "p")
                    if j == 0 and not (isinstance(b, int) and b == 0):
                        for p in parts_stored:
                            dve.wait_ge(p, b * (2 * PUT_COUNT))
                    V.tensor_scalar(g_f, bank_d, gru_b1[:, 1, j:j + 1], None, ALU.add).then_inc(GV, 1)
                elif kind == "in_i":
                    need(dve, gru, "pe", b, s, "p")
                    V.tensor_scalar(g_i, bank_d, gru_b1[:, 2, j:j + 1], None, ALU.add).then_inc(GV, 1)
                elif kind == "g1":
                    need(dve, gru, "dve", b, ("in_i", j), "i")
                    V.scalar_tensor_tensor(g_c, g_f, 0.0, g_i, ALU.min, ALU.min).then_inc(GV, 1)
                elif kind == "g2":
                    need(dve, gru, "act", b, s, "e")
                    V.tensor_tensor(g_fi, g_fi, side[:, 0:1, :].broadcast_to([P, 2, N]), ALU.add).then_inc(GV, 1)
                    need(dve, gru, "dve", b, s, "s")
                    V.tensor_tensor(g_c, g_f, g_i, ALU.add).then_inc(GV, 1)
                elif kind == "g4":
                    need(dve, gru, "act", b, ("g3", j), "rd")
                    V.tensor_tensor(g_i, g_i, g_c, ALU.mult).then_inc(GV, 1)
                    V.tensor_tensor(g_f, g_f, g_c, ALU.mult).then_inc(GV, 1)
                elif kind == "g5":
                    need(dve, gru, "act", b, ("g4", j), "g")
                    V.tensor_tensor(g_r, g_r, g_m, ALU.add).then_inc(GV, 1)
                    need(dve, gru, "dve", b, s, "g")
                    V.tensor_tensor(g_f, g_f, g_r, ALU.mult).then_inc(GV, 1)
                    need(dve, gru, "dve", b, s, "vg")
                    V.tensor_tensor_scan(g_h[j], g_i, g_f, h0[:, j:j + 1], ALU.mult, ALU.add).then_inc(GV, 1)

            def attn_does(l, b, s):
                f, kind = attn[l], s[0]
                FV = f.sem["dve"]
                if kind == "shift":
                    if l:
                        need(dve, post[0], "dve", b, ("y",), "x")
                        need(dve, attn[0], "pe", b, ("v", NT - 1), "p")
                    else:
                        need(dve, pre, "dve", b, ("normed", "in"), "n")
                        need(dve, attn[1], "pe", b - 1, ("v", NT - 1), "p")
                    src = x2 if l else xn0
                    V.tensor_copy(hsh[0:64, :], src[0:64, :])
                    V.tensor_copy(hsh[64:P, 1:], src[64:P, 0:N - 1]).then_inc(FV, 1)
                elif kind == "v":
                    need(dve, f, "pe", b, s, "p")
                    V.tensor_copy(va[:, s[1], :, 0:DH], bank_c.rearrange("p (h d) -> p h d", h=HEADS)).then_inc(FV, 1)
                elif kind == "rot":
                    t = s[1]
                    need(dve, f, "act", b, ("k", t), "sq")
                    V.tensor_reduce(stat[:, 48:64], l_sq.rearrange("p (g d) -> p g d", d=DH), X, ALU.add).then_inc(FV, 1)
                    need(dve, f, "dve", b, s, "ss")
                    if t:
                        need(dve, f, "act", b, ("rot", t - 1), "ln")
                    V.tensor_scalar(stat[:, 0:16], stat[:, 48:64], NORM_LEAST, None, ALU.max).then_inc(FV, 1)
                    need(dve, f, "act", b, ("k", t), "c")
                    if t:
                        need(dve, f, "pool", b, ("rot", t - 1), "add")
                    src = l_qk[t % 2].rearrange("p (k h d) -> p k h d", k=2, d=DH)
                    cos, sin = (tab[:, l, i, t, :, :].unsqueeze(2).broadcast_to([P, 2, HEADS, DH]) for i in range(2))
                    V.tensor_tensor(l_c.rearrange("p (k h d) -> p k h d", k=2, d=DH), src, cos, ALU.mult).then_inc(FV, 1)
                    o = l_s.rearrange("p (k h d) -> p k h d", k=2, d=DH)
                    V.tensor_tensor(o[:, :, :, 0:H], src[:, :, :, H:], sin[:, :, :, 0:H], ALU.mult).then_inc(FV, 1)
                    V.tensor_tensor(o[:, :, :, H:], src[:, :, :, 0:H], sin[:, :, :, H:], ALU.mult).then_inc(FV, 1)
                elif kind == "rot2":
                    t = s[1]
                    need(dve, f, "act", b, ("rot", t), "inv")
                    if t:
                        need(dve, f, "pool", b, ("rot2", t - 1), "q")
                    r, y = stat[:, 32:48], stat[:, 80:96]
                    V.tensor_tensor(y, r, r, ALU.mult).then_inc(FV, 1)
                    need(dve, f, "dve", b, s, "n1")
                    V.tensor_tensor(y, y, stat[:, 0:16], ALU.mult).then_inc(FV, 1)
                    need(dve, f, "dve", b, s, "n2")
                    V.scalar_tensor_tensor(stat[:, 96:112], y, -3.0, r, ALU.add, ALU.mult).then_inc(FV, 1)
                elif kind == "score":
                    u = s[1]
                    need(dve, f, "pe", b, s, "s")
                    sims, top = bank_a.rearrange("p (h n) -> p h n", n=P), stat[:, 64 + 4 * (u % 2):68 + 4 * (u % 2)]
                    V.tensor_reduce(top, sims, X, ALU.max).then_inc(FV, 1)
                    need(dve, f, "dve", b, s, "max")
                    if u >= 2:
                        need(dve, f, "pe", b, ("pturn", u - 2), "t")
                    V.tensor_tensor(prob[u % 2], sims, top.unsqueeze(2).broadcast_to([P, PAIRS, P]), ALU.subtract).then_inc(FV, 1)
                elif kind == "pv":
                    t, par = s[1] // 2, s[1] % 2
                    need(dve, f, "pe", b, s, "o")
                    o = bank_c[:, 0:PAIRS * (DH + 1)].rearrange("p (h d) -> p h d", d=DH + 1)
                    inv = stat[:, 72:76] if par == 0 else stat[:, 76:80]
                    if par == 0 and t:
                        need(dve, f, "pe", b, ("oturn", t - 1), "t")
                    V.reciprocal(inv, o[:, :, DH]).then_inc(FV, 1)
                    need(dve, f, "dve", b, s, "d")
                    V.tensor_tensor(o_row.rearrange("p (h a d) -> p h a d", a=2, h=PAIRS)[:, :, par, :], o[:, :, 0:DH],
                                    inv.unsqueeze(2).broadcast_to([P, PAIRS, DH]), ALU.mult).then_inc(FV, 1)
                elif kind == "wo":
                    t = s[1]
                    need(dve, f, "pe", b, s, "y")
                    if l and t == 0:
                        need(dve, keep1, "pool", b - 1, ("x1",), "c")
                    dst, src = (x3, x2) if l else (x2, xn0)
                    V.tensor_tensor(dst[:, P * t:P * t + P], bank_c[:, 0:P], src[:, P * t:P * t + P], ALU.add).then_inc(FV, 1)

            def post_does(l, b, s):
                f, kind = post[l], s[0]
                FV, xl = f.sem["dve"], x3 if l else x2
                if kind == "shift":
                    need(dve, attn[l], "dve", b, ("wo", NT - 1), "x")
                    if l:
                        need(dve, post[0], "pe", b, ("centre", 0), "c")
                    else:
                        need(dve, post[1], "pe", b - 1, ("centre", 1), "c")
                    V.tensor_copy(mlp_in[0:64, :], xl[0:64, :])
                    V.tensor_copy(mlp_in[64:P, 1:], xl[64:P, 0:N - 1]).then_inc(FV, 1)
                elif kind in NORM_MARKS:
                    norm(f, b, s, xn1[:] if s[1] == "out" else cent[:])
                elif kind == "a":
                    j = s[1]
                    r = ROWS[j]
                    need(dve, f, "pe", b, s, "p")
                    if j == 0:
                        need(dve, f, "act", b, ("gelu",), "g")
                    V.scalar_tensor_tensor(mlp_h[0:r, j, :], (bank_d if l else post0_bank(s))[0:r, :], b1_eff[0:r, l, j:j + 1],
                                           mlp_h[0:r, j, :], ALU.add, ALU.mult).then_inc(FV, 1)
                elif kind == "y":
                    need(dve, f, "pe", b, s, "y")
                    V.scalar_tensor_tensor(xl[:], bank_d if l else post0_bank(s), mlp_b2[:, l:l + 1], xl[:], ALU.add, ALU.add).then_inc(FV, 1)
                elif kind == "silu1":
                    need(dve, f, "dve", b, ("y",), "x")
                    need(dve, gru, "dve", b, ("g5", JG - 1), "h")
                    V.scalar_tensor_tensor(s_sig, x3[:], -1.0, x3[:], ALU.mult, ALU.min).then_inc(FV, 1)
                elif kind == "silu2":
                    need(dve, f, "act", b, ("silu1",), "l")
                    V.scalar_tensor_tensor(s_sig, x3[:], 0.0, s_sig, ALU.min, ALU.subtract).then_inc(FV, 1)
                elif kind == "silu3":
                    need(dve, f, "act", b, ("silu2",), "s")
                    V.tensor_tensor(x3[:], x3[:], s_sig, ALU.mult).then_inc(FV, 1)
                elif kind == "qk":
                    c = s[1]
                    need(dve, f, "act", b, s, "p0")
                    scale = K1 ** -0.5 if c < 2 else 1.0
                    V.scalar_tensor_tensor(rest[c % 2], bank_d, scale, parts[:, c % 2, 0, :], ALU.mult, ALU.subtract).then_inc(FV, 1)
                elif kind == "qk2":
                    c = s[1]
                    need(dve, f, "act", b, s, "p1")
                    V.tensor_tensor(parts[:, c % 2, 2, :], rest[c % 2], parts[:, c % 2, 1, :], ALU.subtract).then_inc(FV, 1)

            def glob_does(b, s):
                kind, GV = s[0], glob.sem["dve"]
                if kind == "sim":
                    _, h, m = s
                    c = 4 * h + m
                    need(dve, glob, "pe", b, s, "s")
                    V.tensor_reduce(nmax[:, c % 8:c % 8 + 1], s_bank[c % 2][:], X, ALU.max, negate=True).then_inc(GV, 1)
                elif kind == "scale_v":
                    h = s[1]
                    need(dve, glob, "act", b, ("sim", h, 3), "e")
                    if h >= 2:
                        need(dve, glob, "pool", b, ("scale_v", h - 2), "v")
                    else:
                        need(dve, glob, "pool", b - 1, ("scale_v", H1 - 2 + h), "v")
                    V.reciprocal(rinv[:, h % 2, :], rsum[:, h % 2, :]).then_inc(GV, 1)
                elif kind == "gate":
                    need(dve, glob, "pe", b, ("proj", 7), "y")
                    need(dve, glob, "pool", b - 1, ("gate",), "g")
                    V.tensor_tensor(yf, y_bank[:], gate[:], ALU.mult).then_inc(GV, 1)

            def expert():
                dve.wait_ge(routing_loaded, 32)
                V.tensor_copy(ehf, eidx).then_inc(prep_dve, 1)
                dve.wait_ge(prep_dve, 5)
                for e in range(E):
                    V.scalar_tensor_tensor(etmp[:, e], ehf, float(e), ews, ALU.is_equal, ALU.mult).then_inc(prep_dve, 1)
                dve.wait_ge(prep_dve, 5 + E)
                V.tensor_reduce(ewt, etmp, X, ALU.add).then_inc(prep_dve, 1)
                dve.wait_ge(prep_dve, 6 + E)
                n = 0
                for e in range(E):
                    for t in range(NT):
                        dve.wait_ge(expert_pe, 8 * e + JF + t + 1)
                        src = s_bank[n % 2][:, 0:P]
                        if e == 0:
                            V.tensor_scalar(eacc[:, t, :], src, ewt[:, e, t:t + 1], None, ALU.mult).then_inc(expert_dve, 1)
                        else:
                            dve.wait_ge(expert_dve, n - NT + 1)
                            V.scalar_tensor_tensor(eacc[:, t, :], src, ewt[:, e, t:t + 1], eacc[:, t, :], ALU.mult, ALU.add)\
                                .then_inc(expert_dve, 1)
                        n += 1
                dve.wait_ge(expert_pe, 8 * E + 1)
                V.tensor_scalar(es[0], y_bank[:], bias1, None, ALU.add).then_inc(expert_dve, 1)
                dve.wait_ge(expert_dve, n + 1)
                V.scalar_tensor_tensor(es[1], es[0], -1.0, es[0], ALU.mult, ALU.min).then_inc(expert_dve, 1)
                dve.wait_ge(expert_act, E * JF + 2)
                V.scalar_tensor_tensor(es[3], es[0], 0.0, es[2], ALU.min, ALU.subtract).then_inc(expert_dve, 1)
                dve.wait_ge(expert_act, E * JF + 3)
                V.tensor_tensor(gate[:], es[0], es[3], ALU.mult).then_inc(expert_dve, 1)

            run(dve, "dve", {
                "pre": pre_does, "gru": gru_does, "glob": glob_does,
                "attn0": lambda b, s: attn_does(0, b, s), "attn1": lambda b, s: attn_does(1, b, s),
                "post0": lambda b, s: post_does(0, b, s), "post1": lambda b, s: post_does(1, b, s)}, expert)

        @block.gpsimd
        def _(pool):
            G = nc.gpsimd
            G.memset(eps, EPS)
            G.memset(one, 1.0)
            G.memset(norm_bias, float(0.5 * NORM_SHIFT * np.log(2.0)))
            G.memset(hsh[:, 0:1], 0.0)
            G.memset(mlp_in[:, 0:1], 0.0)
            G.memset(kT[:, :, 0:WIN], 0.0)
            G.memset(va[:, :, :, DH:], 1.0)
            G.memset(vb[:, 0, :, 0:DH], 0.0)
            G.memset(vb[:, :, :, DH:], 1.0).then_inc(prep_pool, 1)

            def gru_does(b, s):
                j, GP = s[1], gru.sem["pool"]
                if s[0] == "g1":
                    need(pool, gru, "dve", b, s, "c")
                    G.tensor_tensor(g_f, g_c, g_f, ALU.subtract).then_inc(GP, 1)
                    G.tensor_tensor(g_i, g_c, g_i, ALU.subtract).then_inc(GP, 1)
                else:
                    need(pool, gru, "act", b, ("g2", j), "lm")
                    G.tensor_tensor(g_m, g_m, sq[:], ALU.subtract).then_inc(GP, 1)

            def attn_does(l, b, s):
                f, t = attn[l], s[1]
                if s[0] == "rot":
                    need(pool, f, "dve", b, s, "s1")
                    if t:
                        need(pool, f, "pe", b, ("tk", t - 1), "t")
                    G.tensor_tensor(l_q, l_c, l_s, ALU.add).then_inc(f.sem["pool"], 1)
                    return
                need(pool, f, "pool", b, ("rot", t), "add")
                need(pool, f, "dve", b, s, "inv")
                q = l_q.rearrange("p (g d) -> p g d", d=DH)
                G.tensor_tensor(q, q, stat[:, 96:112].unsqueeze(2).broadcast_to([P, 2 * HEADS, DH]), ALU.mult)\
                    .then_inc(f.sem["pool"], 1)

            def post_does(b, s):
                FP = post[1].sem["pool"]
                need(pool, post[1], "dve", b, s, "y")
                need(pool, gru, "act", b, ("out",), "o")
                G.tensor_tensor(s_g, x3[:], gru_o[:], ALU.mult).then_inc(FP, 1)
                need(pool, post[1], "pool", b, s, "g")
                need(pool, keep0, "pool", b, ("x0",), "c")
                G.tensor_tensor(x3[:], s_g, x0[:], ALU.add).then_inc(FP, 1)

            def keep0_does(b, s):
                need(pool, pre, "act", b, ("x",), "x")
                need(pool, post[1], "pool", b - 1, ("silu3",), "x")
                G.tensor_tensor(x0[:], x_new[:], one.to_broadcast([P, N]), ALU.mult).then_inc(keep0.sem["pool"], 1)

            def keep1_does(b, s):
                need(pool, post[1], "pool", b, ("silu3",), "x")
                need(pool, glob, "pool", b - 1, ("gate",), "x")
                G.tensor_tensor(x1[:], x3[:], one.to_broadcast([P, N]), ALU.mult).then_inc(keep1.sem["pool"], 1)

            def glob_does(b, s):
                GP = glob.sem["pool"]
                if s[0] == "scale_v":
                    h = s[1]
                    need(pool, glob, "dve", b, s, "r")
                    if h == 0:
                        need(pool, glob, "act", b, ("values", 2 * NT - 1), "v")
                    if h >= 2:
                        need(pool, glob, "pe", b, ("av", h - 2), "o")
                    else:
                        need(pool, glob, "pe", b - 1, ("av", H1 - 2 + h), "o")
                    G.tensor_tensor(vsc[:, h % 2], vrow[:, :, V1 * h:V1 * h + V1],
                                    rinv[:, h % 2, :].unsqueeze(2).broadcast_to([P, 4, V1]), ALU.mult).then_inc(GP, 1)
                elif s[0] == "gate":
                    need(pool, glob, "dve", b, s, "g")
                    need(pool, keep1, "pool", b, ("x1",), "c")
                    G.tensor_tensor(yf, yf, x1[:], ALU.add).then_inc(GP, 1)
                    G.tensor_copy(gate[:], gate1.to_broadcast([P, N])).then_inc(GP, 1)

            def expert():
                need(pool, attn[0], "dve", 1, ("wo", NT - 1), "x")
                pool.dma_start(eidx, a["L1_ffn_expert_indices"].rearrange("(t p) k -> p t k", p=P)).then_inc(routing_loaded, 16)
                pool.dma_start(ews, a["L1_ffn_expert_weights"].rearrange("(t p) k -> p t k", p=P)).then_inc(routing_loaded, 16)

            run(pool, "pool", {
                "gru": gru_does, "glob": glob_does, "post1": post_does, "keep0": keep0_does, "keep1": keep1_does,
                "attn0": lambda b, s: attn_does(0, b, s), "attn1": lambda b, s: attn_does(1, b, s)}, expert)


_INS = ["L0_attn_x", "L0_attn_W1", "L0_attn_b1", "L0_attn_W2", "L0_attn_b2", "L0_attn_init_h", "L0_ffn_wqkv",
        "L0_ffn_q_scale", "L0_ffn_k_scale", "L0_ffn_wo", "L0_ffn_ln_g", "L0_ffn_ln_b", "L0_ffn_w1", "L0_ffn_b1",
        "L0_ffn_w2", "L0_ffn_b2", "L1_attn_query_proj", "L1_attn_key_proj", "L1_attn_value_proj",
        "L1_attn_output_proj", "L1_ffn_expert_weights", "L1_ffn_expert_indices", "L1_ffn_w1", "L1_ffn_w2",
        "L1_ffn_bias"]


def kernel(**inputs):
    import concourse.bacc as bacc
    from concourse.bass_utils import run_bass_kernel_spmd as launch

    nc = bacc.Bacc("TRN2", target_bir_lowering=False, num_devices=1)
    arrays = {n: np.ascontiguousarray(inputs[n]) for n in _INS}
    arrays["const"] = constants()
    aps = {n: nc.dram_tensor(f"in_{n}", v.shape, mybir.dt.from_np(v.dtype), kind="ExternalInput").ap()
           for n, v in arrays.items()}
    out = nc.dram_tensor("out", (B, N, D), F32, kind="ExternalOutput").ap()
    build(nc, aps, out)
    r = launch(nc, [{f"in_{n}": v for n, v in arrays.items()}], core_ids=[0])
    return r.results[0]["out"]
```
